# Optimizing a Trainium2 kernel written in Bass

```python
import numpy as np
import jax
import jax.numpy as jnp

def _softmax(x, axis=-1):
    return jax.nn.softmax(x, axis=axis)

def _gelu(x):
    return jax.nn.gelu(x, approximate=True)

def _silu(x):
    return jax.nn.silu(x)

def _sigmoid(x):
    return jax.nn.sigmoid(x)

def _layernorm(x, axis=-1, eps=1e-05):
    m = jnp.mean(x, axis=axis, keepdims=True)
    v = jnp.var(x, axis=axis, keepdims=True)
    return (x - m) / jnp.sqrt(v + eps)

def _scatter_add(tgt, idx, src, axis=0):
    return tgt.at[idx].add(src)

def _segment_sum(src, seg, n):
    return jax.ops.segment_sum(src, seg, n)
kernel_name = 'mk_decoder_postln_d2_seqx_r4_8547bf'

def setup_inputs(seed: int=0):
    np.random.seed(seed)
    _w = jnp.asarray

    def _rec_inputs():
        import jax
        import jax.numpy as jnp
        _rk = jax.random.key(seed)
        x = -0.0002928 + 1 * jax.random.normal(jax.random.fold_in(_rk, 1), (1, 2048, 256), jnp.float32)
        _lenS = 2048 - jax.random.randint(jax.random.fold_in(_rk, 7), (1,), 0, max(1, 2048 // 4) + 1, jnp.int32)
        _lenS2 = 1601 - jax.random.randint(jax.random.fold_in(_rk, 8), (1,), 0, max(1, 1601 // 4) + 1, jnp.int32)
        _ctx_1024P = jax.random.normal(jax.random.fold_in(_rk, 11), (1, 16, 256), jnp.float32)
        _ctx_1024c = jax.random.dirichlet(jax.random.fold_in(_rk, 511), 0.3 * jnp.ones((16,), jnp.float32), (1, 1601))
        _ctx_1024t = jnp.einsum('bsk,bkd->bsd', _ctx_1024c, _ctx_1024P)
        _ctx_1024t = _ctx_1024t * jax.lax.rsqrt(jnp.mean(jnp.square(_ctx_1024t)) + 1e-12) * 0.953939
        ctx_1024 = -1.39393e-06 + 0.999914 * (_ctx_1024t + 0.3 * jax.random.normal(jax.random.fold_in(_rk, 611), (1, 1601, 256), jnp.float32))
        _validS = jnp.arange(2048)[None, :] < _lenS[:, None]
        _validS2 = jnp.arange(1601)[None, :] < _lenS2[:, None]
        _causal = jnp.tril(jnp.ones((2048, 2048), dtype=bool))
        mask_1x1xSxS2_ff0 = jnp.where(jnp.ones((1, 1, 2048, 1601), dtype=bool), 0.0, -1000000000.0).astype(jnp.float32)
        mask_BxS2_bk0 = jnp.logical_not(jnp.broadcast_to(_validS2[:, :], (1, 1601)))
        return (x, ctx_1024, mask_1x1xSxS2_ff0, mask_BxS2_bk0)
    x, ctx_1024, mask_1x1xSxS2_ff0, mask_BxS2_bk0 = _rec_inputs()

    def _L0_attn_setup():
        import math
        import jax, jax.numpy as jnp
        import numpy as np
        D_MODEL = 256
        HEADS = 16
        DH = D_MODEL // HEADS
        MAX_REL = 128
        LN_EPS = 1e-05

        def _layernorm(x, gamma, beta):
            mu = jnp.mean(x, axis=-1, keepdims=True)
            var = jnp.mean(jnp.square(x - mu), axis=-1, keepdims=True)
            return (x - mu) * jax.lax.rsqrt(var + LN_EPS) * gamma + beta
        key = jax.random.key(seed)
        ks = jax.random.split(key, 6)
        B, T = (4, 512)
        scale = 1.0 / math.sqrt(D_MODEL)
        x = jax.random.normal(ks[0], (B, T, D_MODEL), dtype=jnp.float32)
        Wq = jax.random.normal(ks[1], (D_MODEL, D_MODEL), dtype=jnp.float32) * scale
        Wk = jax.random.normal(ks[2], (D_MODEL, D_MODEL), dtype=jnp.float32) * scale
        Wv = jax.random.normal(ks[3], (D_MODEL, D_MODEL), dtype=jnp.float32) * scale
        Wo = jax.random.normal(ks[4], (D_MODEL, D_MODEL), dtype=jnp.float32) * scale
        rel = jnp.tile(jnp.linspace(0.0, -2.0, MAX_REL + 1, dtype=jnp.float32)[None, :], (HEADS, 1))
        ln_gamma = jnp.ones((D_MODEL,), dtype=jnp.float32)
        ln_beta = jnp.zeros((D_MODEL,), dtype=jnp.float32)
        return {'x': x, 'Wq': Wq, 'Wk': Wk, 'Wv': Wv, 'Wo': Wo, 'rel': rel, 'ln_gamma': ln_gamma, 'ln_beta': ln_beta}
    _L0_attn_all = _L0_attn_setup()
    _L0_attn_in = {k: v for k, v in _L0_attn_all.items() if k in ('Wq', 'Wk', 'Wv', 'Wo', 'rel', 'ln_gamma', 'ln_beta')}
    del _L0_attn_all

    def _L0_xattn_setup():
        import jax, jax.numpy as jnp
        import numpy as np
        D_MODEL = 256
        NUM_HEADS = 16
        DEPTH = D_MODEL // NUM_HEADS
        B, S = (2, 512)

        def _split_heads(x):
            b, s, _ = x.shape
            return x.reshape(b, s, NUM_HEADS, DEPTH).transpose(0, 2, 1, 3)
        key = jax.random.key(seed)
        ks = jax.random.split(key, 12)
        scale = 1.0 / np.sqrt(D_MODEL)
        inp = {'q': jax.random.normal(ks[0], (B, S, D_MODEL), dtype=jnp.float32), 'k': jax.random.normal(ks[1], (B, S, D_MODEL), dtype=jnp.float32), 'v': jax.random.normal(ks[2], (B, S, D_MODEL), dtype=jnp.float32), 'mask': jnp.zeros((1, 1, S, S), dtype=jnp.float32), 'wq': jax.random.normal(ks[3], (D_MODEL, D_MODEL), dtype=jnp.float32) * scale, 'bq': jnp.zeros((D_MODEL,), dtype=jnp.float32), 'wk': jax.random.normal(ks[4], (D_MODEL, D_MODEL), dtype=jnp.float32) * scale, 'bk': jnp.zeros((D_MODEL,), dtype=jnp.float32), 'wv': jax.random.normal(ks[5], (D_MODEL, D_MODEL), dtype=jnp.float32) * scale, 'bv': jnp.zeros((D_MODEL,), dtype=jnp.float32), 'wo': jax.random.normal(ks[6], (D_MODEL, D_MODEL), dtype=jnp.float32) * scale, 'bo': jnp.zeros((D_MODEL,), dtype=jnp.float32)}
        return inp
    _L0_xattn_all = _L0_xattn_setup()
    _L0_xattn_in = {k: v for k, v in _L0_xattn_all.items() if k in ('wq', 'bq', 'wk', 'bk', 'wv', 'bv', 'wo', 'bo')}
    del _L0_xattn_all

    def _L0_ffn_setup():
        import jax, jax.numpy as jnp
        import numpy as np
        BLOCK = 32
        W_BITS = 4
        ACT_BITS = 16

        def act_qdq(x):
            qmax = 2.0 ** (ACT_BITS - 1) - 1.0
            scale = jnp.maximum(jnp.max(jnp.abs(x)) / qmax, 1e-12)
            return jnp.clip(jnp.round(x / scale), -qmax - 1.0, qmax) * scale

        def fixed_qdq_u16(x):
            scale = 1.0 / 65536.0
            return jnp.clip(jnp.round(x / scale), 0.0, 65535.0) * scale

        def lpbq_dequant(w):
            O, I = w.shape
            qmax = 2.0 ** (W_BITS - 1) - 1.0
            wb = w.reshape(O, I // BLOCK, BLOCK)
            s = jnp.maximum(jnp.max(jnp.abs(wb), axis=-1, keepdims=True) / qmax, 1e-12)
            wq = jnp.clip(jnp.round(wb / s), -qmax - 1.0, qmax) * s
            return wq.reshape(O, I)
        key = jax.random.key(seed)
        k1, k2, k3, k4 = jax.random.split(key, 4)
        B, S, H, I = (2, 1024, 256, 768)
        x = jax.random.normal(k1, (B, S, H), jnp.float32)
        w_gate = jax.random.normal(k2, (I, H), jnp.float32) * 0.02
        w_up = jax.random.normal(k3, (I, H), jnp.float32) * 0.02
        w_down = jax.random.normal(k4, (H, I), jnp.float32) * 0.02
        return {'x': x, 'w_gate': w_gate, 'w_up': w_up, 'w_down': w_down}
    _L0_ffn_all = _L0_ffn_setup()
    _L0_ffn_in = {k: v for k, v in _L0_ffn_all.items() if k in ('w_gate', 'w_up', 'w_down')}
    del _L0_ffn_all

    def _L1_attn_setup():
        import jax, jax.numpy as jnp
        import numpy as np
        D_MODEL = 256
        NUM_HEADS = 16
        D_HEAD = D_MODEL // NUM_HEADS
        key = jax.random.key(seed)
        ks = jax.random.split(key, 5)
        b, n = (4, 512)
        x = jax.random.normal(ks[0], (b, n, D_MODEL), dtype=jnp.float32)
        s = 1.0 / np.sqrt(D_MODEL)
        w_qkv = jax.random.normal(ks[1], (D_MODEL, 3 * D_MODEL), dtype=jnp.float32) * s
        b_qkv = jax.random.normal(ks[2], (3 * D_MODEL,), dtype=jnp.float32) * 0.01
        w_out = jax.random.normal(ks[3], (D_MODEL, D_MODEL), dtype=jnp.float32) * s
        b_out = jax.random.normal(ks[4], (D_MODEL,), dtype=jnp.float32) * 0.01
        return {'x': x, 'w_qkv': w_qkv, 'b_qkv': b_qkv, 'w_out': w_out, 'b_out': b_out}
    _L1_attn_all = _L1_attn_setup()
    _L1_attn_in = {k: v for k, v in _L1_attn_all.items() if k in ('w_qkv', 'b_qkv', 'w_out', 'b_out')}
    del _L1_attn_all

    def _L1_xattn_setup():
        import jax, jax.numpy as jnp
        import numpy as np
        NUM_HEADS = 16
        EPS = 1e-06

        def _ln(t, w, b):
            mu = jnp.mean(t, axis=-1, keepdims=True)
            var = jnp.mean(jnp.square(t - mu), axis=-1, keepdims=True)
            return (t - mu) * jax.lax.rsqrt(var + EPS) * w + b
        key = jax.random.key(seed)
        ks = jax.random.split(key, 10)
        b, s1, s2, qdim, kdim = (2, 512, 768, 256, 256)
        d = qdim // NUM_HEADS
        x = jax.random.normal(ks[0], (b, s1, qdim), dtype=jnp.float32)
        y = jax.random.normal(ks[1], (b, s2, kdim), dtype=jnp.float32)
        padding_mask = jax.random.randint(ks[2], (b, s2), 0, 2) > 0
        padding_mask = padding_mask.at[:, 0].set(True)
        w = 0.02
        Wq = jax.random.normal(ks[3], (qdim, qdim), dtype=jnp.float32) * w
        bq = jnp.zeros((qdim,), jnp.float32)
        Wkv = jax.random.normal(ks[4], (2 * qdim, kdim), dtype=jnp.float32) * w
        bkv = jnp.zeros((2 * qdim,), jnp.float32)
        qn_w = jnp.ones((d,), jnp.float32)
        qn_b = jnp.zeros((d,), jnp.float32)
        kn_w = jnp.ones((d,), jnp.float32)
        kn_b = jnp.zeros((d,), jnp.float32)
        Wo = jax.random.normal(ks[5], (qdim, qdim), dtype=jnp.float32) * w
        bo = jnp.zeros((qdim,), jnp.float32)
        return {'x': x, 'y': y, 'padding_mask': padding_mask, 'Wq': Wq, 'bq': bq, 'Wkv': Wkv, 'bkv': bkv, 'qn_w': qn_w, 'qn_b': qn_b, 'kn_w': kn_w, 'kn_b': kn_b, 'Wo': Wo, 'bo': bo}
    _L1_xattn_all = _L1_xattn_setup()
    _L1_xattn_in = {k: v for k, v in _L1_xattn_all.items() if k in ('Wq', 'bq', 'Wkv', 'bkv', 'qn_w', 'qn_b', 'kn_w', 'kn_b', 'Wo', 'bo')}
    del _L1_xattn_all

    def _L1_ffn_setup():
        import jax, jax.numpy as jnp
        import numpy as np
        CAPACITY_FACTOR = 1.0

        def _route(token_inputs, Wg, capacity):
            dt = token_inputs.dtype
            logits = jnp.einsum('bnd,de->bne', token_inputs, Wg)
            gates = jax.nn.softmax(logits, axis=-1)
            expert_idx = jnp.argmax(gates, axis=-1)
            mask = jax.nn.one_hot(expert_idx, Wg.shape[1], dtype=dt)
            gate = jnp.sum(gates * mask, axis=-1)
            pos = jnp.cumsum(mask, axis=1) * mask - mask
            keep = mask * (pos < capacity).astype(dt)
            pos_oh = jax.nn.one_hot(pos.astype(jnp.int32), capacity, dtype=dt)
            dispatch = keep[..., None] * pos_oh
            combine = dispatch * gate[:, :, None, None]
            return (dispatch, combine)
        key = jax.random.key(seed)
        k1, k2, k3, k4 = jax.random.split(key, 4)
        B, N, D, E, H = (8, 512, 256, 8, 1024)
        return {'token_inputs': jax.random.normal(k1, (B, N, D), dtype=jnp.float32), 'Wg': jax.random.normal(k2, (D, E), dtype=jnp.float32) * 0.02, 'W1': jax.random.normal(k3, (E, D, H), dtype=jnp.float32) * 0.02, 'W2': jax.random.normal(k4, (E, H, D), dtype=jnp.float32) * 0.02}
    _L1_ffn_all = _L1_ffn_setup()
    _L1_ffn_in = {k: v for k, v in _L1_ffn_all.items() if k in ('Wg', 'W1', 'W2')}
    del _L1_ffn_all
    return {'x': x, 'ctx_1024': ctx_1024, 'mask_1x1xSxS2_ff0': mask_1x1xSxS2_ff0, 'mask_BxS2_bk0': mask_BxS2_bk0, 'L0_attn_Wq': _L0_attn_in['Wq'], 'L0_attn_Wk': _L0_attn_in['Wk'], 'L0_attn_Wv': _L0_attn_in['Wv'], 'L0_attn_Wo': _L0_attn_in['Wo'], 'L0_attn_rel': _L0_attn_in['rel'], 'L0_attn_ln_gamma': _L0_attn_in['ln_gamma'], 'L0_attn_ln_beta': _L0_attn_in['ln_beta'], 'L0_xattn_wq': _L0_xattn_in['wq'], 'L0_xattn_bq': _L0_xattn_in['bq'], 'L0_xattn_wk': _L0_xattn_in['wk'], 'L0_xattn_bk': _L0_xattn_in['bk'], 'L0_xattn_wv': _L0_xattn_in['wv'], 'L0_xattn_bv': _L0_xattn_in['bv'], 'L0_xattn_wo': _L0_xattn_in['wo'], 'L0_xattn_bo': _L0_xattn_in['bo'], 'L0_ffn_w_gate': _L0_ffn_in['w_gate'], 'L0_ffn_w_up': _L0_ffn_in['w_up'], 'L0_ffn_w_down': _L0_ffn_in['w_down'], 'L1_attn_w_qkv': _L1_attn_in['w_qkv'], 'L1_attn_b_qkv': _L1_attn_in['b_qkv'], 'L1_attn_w_out': _L1_attn_in['w_out'], 'L1_attn_b_out': _L1_attn_in['b_out'], 'L1_xattn_Wq': _L1_xattn_in['Wq'], 'L1_xattn_bq': _L1_xattn_in['bq'], 'L1_xattn_Wkv': _L1_xattn_in['Wkv'], 'L1_xattn_bkv': _L1_xattn_in['bkv'], 'L1_xattn_qn_w': _L1_xattn_in['qn_w'], 'L1_xattn_qn_b': _L1_xattn_in['qn_b'], 'L1_xattn_kn_w': _L1_xattn_in['kn_w'], 'L1_xattn_kn_b': _L1_xattn_in['kn_b'], 'L1_xattn_Wo': _L1_xattn_in['Wo'], 'L1_xattn_bo': _L1_xattn_in['bo'], 'L1_ffn_Wg': _L1_ffn_in['Wg'], 'L1_ffn_W1': _L1_ffn_in['W1'], 'L1_ffn_W2': _L1_ffn_in['W2']}

def reference(x, ctx_1024, mask_1x1xSxS2_ff0, mask_BxS2_bk0, L0_attn_Wq, L0_attn_Wk, L0_attn_Wv, L0_attn_Wo, L0_attn_rel, L0_attn_ln_gamma, L0_attn_ln_beta, L0_xattn_wq, L0_xattn_bq, L0_xattn_wk, L0_xattn_bk, L0_xattn_wv, L0_xattn_bv, L0_xattn_wo, L0_xattn_bo, L0_ffn_w_gate, L0_ffn_w_up, L0_ffn_w_down, L1_attn_w_qkv, L1_attn_b_qkv, L1_attn_w_out, L1_attn_b_out, L1_xattn_Wq, L1_xattn_bq, L1_xattn_Wkv, L1_xattn_bkv, L1_xattn_qn_w, L1_xattn_qn_b, L1_xattn_kn_w, L1_xattn_kn_b, L1_xattn_Wo, L1_xattn_bo, L1_ffn_Wg, L1_ffn_W1, L1_ffn_W2):
    import jax
    import jax.numpy as jnp

    def _L0_attn_ref(x, Wq, Wk, Wv, Wo, rel, ln_gamma, ln_beta):
        import math
        import jax, jax.numpy as jnp
        import numpy as np
        D_MODEL = 256
        HEADS = 16
        DH = D_MODEL // HEADS
        MAX_REL = 128
        LN_EPS = 1e-05

        def _layernorm(x, gamma, beta):
            mu = jnp.mean(x, axis=-1, keepdims=True)
            var = jnp.mean(jnp.square(x - mu), axis=-1, keepdims=True)
            return (x - mu) * jax.lax.rsqrt(var + LN_EPS) * gamma + beta
        B, T, D = x.shape
        x0 = x
        xn = _layernorm(x, ln_gamma, ln_beta)

        def proj(W):
            return (xn @ W.T).reshape(B, T, HEADS, DH).transpose(0, 2, 1, 3)
        q = proj(Wq) / math.sqrt(DH)
        k = proj(Wk)
        v = proj(Wv)
        scores = jnp.einsum('bhid,bhjd->bhij', q, k)
        i = jnp.arange(T)
        dist = jnp.clip(i[:, None] - i[None, :], 0, MAX_REL)
        bias = rel[:, dist]
        scores = scores + bias[None]
        causal = i[:, None] >= i[None, :]
        scores = jnp.where(causal[None, None], scores, -jnp.inf)
        attn = jax.nn.softmax(scores, axis=-1)
        y = jnp.einsum('bhij,bhjd->bhid', attn, v)
        y = y.transpose(0, 2, 1, 3).reshape(B, T, D)
        y = y @ Wo.T
        return x0 + y

    def _L0_xattn_ref(q, k, v, mask, wq, bq, wk, bk, wv, bv, wo, bo):
        import jax, jax.numpy as jnp
        import numpy as np
        D_MODEL = 256
        NUM_HEADS = 16
        DEPTH = D_MODEL // NUM_HEADS
        B, S = (2, 512)

        def _split_heads(x):
            b, s, _ = x.shape
            return x.reshape(b, s, NUM_HEADS, DEPTH).transpose(0, 2, 1, 3)
        qh = _split_heads(q @ wq + bq)
        kh = _split_heads(k @ wk + bk)
        vh = _split_heads(v @ wv + bv)
        logits = jnp.einsum('bhqd,bhkd->bhqk', qh, kh) / jnp.sqrt(jnp.float32(DEPTH))
        logits = logits + mask * -1000000000.0
        attn = jax.nn.softmax(logits, axis=-1)
        out = jnp.einsum('bhqk,bhkd->bhqd', attn, vh)
        out = out.transpose(0, 2, 1, 3).reshape(q.shape[0], -1, D_MODEL)
        return out @ wo + bo

    def _L0_ffn_ref(x, w_gate, w_up, w_down):
        import jax, jax.numpy as jnp
        import numpy as np
        BLOCK = 32
        W_BITS = 4
        ACT_BITS = 16

        def act_qdq(x):
            qmax = 2.0 ** (ACT_BITS - 1) - 1.0
            scale = jnp.maximum(jnp.max(jnp.abs(x)) / qmax, 1e-12)
            return jnp.clip(jnp.round(x / scale), -qmax - 1.0, qmax) * scale

        def fixed_qdq_u16(x):
            scale = 1.0 / 65536.0
            return jnp.clip(jnp.round(x / scale), 0.0, 65535.0) * scale

        def lpbq_dequant(w):
            O, I = w.shape
            qmax = 2.0 ** (W_BITS - 1) - 1.0
            wb = w.reshape(O, I // BLOCK, BLOCK)
            s = jnp.maximum(jnp.max(jnp.abs(wb), axis=-1, keepdims=True) / qmax, 1e-12)
            wq = jnp.clip(jnp.round(wb / s), -qmax - 1.0, qmax) * s
            return wq.reshape(O, I)
        x = act_qdq(x)
        up = act_qdq(x @ lpbq_dequant(w_up).T)
        gate = act_qdq(x @ lpbq_dequant(w_gate).T)
        sig = fixed_qdq_u16(jax.nn.sigmoid(gate))
        gate = act_qdq(gate * sig)
        o = act_qdq(gate * up)
        return o @ lpbq_dequant(w_down).T

    def _L1_attn_ref(x, w_qkv, b_qkv, w_out, b_out):
        import jax, jax.numpy as jnp
        import numpy as np
        D_MODEL = 256
        NUM_HEADS = 16
        D_HEAD = D_MODEL // NUM_HEADS
        b, n, _ = x.shape
        h, d = (NUM_HEADS, D_HEAD)
        scale = d ** (-0.5)
        qkv = x @ w_qkv + b_qkv
        qkv = qkv.reshape(b, n, 3, h, d).transpose(2, 0, 3, 1, 4)
        q, k, v = (qkv[0], qkv[1], qkv[2])
        dots = jnp.einsum('bhid,bhjd->bhij', q, k) * scale
        causal = jnp.tril(jnp.ones((n, n), dtype=bool))
        dots = jnp.where(causal[None, None], dots, -jnp.inf)
        attn = jax.nn.softmax(dots, axis=-1)
        out = jnp.einsum('bhij,bhjd->bhid', attn, v)
        out = out.transpose(0, 2, 1, 3).reshape(b, n, h * d)
        return out @ w_out + b_out

    def _L1_xattn_ref(x, y, padding_mask, Wq, bq, Wkv, bkv, qn_w, qn_b, kn_w, kn_b, Wo, bo):
        import jax, jax.numpy as jnp
        import numpy as np
        NUM_HEADS = 16
        EPS = 1e-06

        def _ln(t, w, b):
            mu = jnp.mean(t, axis=-1, keepdims=True)
            var = jnp.mean(jnp.square(t - mu), axis=-1, keepdims=True)
            return (t - mu) * jax.lax.rsqrt(var + EPS) * w + b
        b, s1, c = x.shape
        s2 = y.shape[1]
        h, d = (NUM_HEADS, c // NUM_HEADS)
        scale = d ** (-0.5)
        q = (x @ Wq.T + bq).reshape(b, s1, h, d)
        kv = (y @ Wkv.T + bkv).reshape(b, s2, 2, h, d)
        k, v = (kv[:, :, 0], kv[:, :, 1])
        q = _ln(q, qn_w, qn_b) * scale
        k = _ln(k, kn_w, kn_b)
        attn = jnp.einsum('bihd,bjhd->bhij', q, k)
        attn = jnp.where(padding_mask[:, None, None, :], attn, -jnp.inf)
        p = jax.nn.softmax(attn, axis=-1)
        ctx = jnp.einsum('bhij,bjhd->bihd', p, v).reshape(b, s1, c)
        out = ctx @ Wo.T + bo
        return out

    def _L1_ffn_ref(token_inputs, Wg, W1, W2):
        import jax, jax.numpy as jnp
        import numpy as np
        CAPACITY_FACTOR = 1.0

        def _route(token_inputs, Wg, capacity):
            dt = token_inputs.dtype
            logits = jnp.einsum('bnd,de->bne', token_inputs, Wg)
            gates = jax.nn.softmax(logits, axis=-1)
            expert_idx = jnp.argmax(gates, axis=-1)
            mask = jax.nn.one_hot(expert_idx, Wg.shape[1], dtype=dt)
            gate = jnp.sum(gates * mask, axis=-1)
            pos = jnp.cumsum(mask, axis=1) * mask - mask
            keep = mask * (pos < capacity).astype(dt)
            pos_oh = jax.nn.one_hot(pos.astype(jnp.int32), capacity, dtype=dt)
            dispatch = keep[..., None] * pos_oh
            combine = dispatch * gate[:, :, None, None]
            return (dispatch, combine)
        B, N, D = token_inputs.shape
        E = Wg.shape[1]
        capacity = int(N * CAPACITY_FACTOR // E)
        dispatch, combine = _route(token_inputs, Wg, capacity)
        expert_inputs = jnp.einsum('bnd,bnec->becd', token_inputs, dispatch)
        h = jax.nn.gelu(jnp.einsum('becd,edh->bech', expert_inputs, W1))
        expert_outputs = jnp.einsum('bech,ehd->becd', h, W2)
        output = jnp.einsum('becd,bnec->bnd', expert_outputs, combine)
        return output
    x = _layernorm(x + _L0_attn_ref(x, L0_attn_Wq, L0_attn_Wk, L0_attn_Wv, L0_attn_Wo, L0_attn_rel, L0_attn_ln_gamma, L0_attn_ln_beta), axis=-1)
    x = _layernorm(x + _L0_xattn_ref(x, ctx_1024, ctx_1024, mask_1x1xSxS2_ff0, L0_xattn_wq, L0_xattn_bq, L0_xattn_wk, L0_xattn_bk, L0_xattn_wv, L0_xattn_bv, L0_xattn_wo, L0_xattn_bo), axis=-1)
    x = _layernorm(x + _L0_ffn_ref(x, L0_ffn_w_gate, L0_ffn_w_up, L0_ffn_w_down), axis=-1)
    x = _layernorm(x + _L1_attn_ref(x, L1_attn_w_qkv, L1_attn_b_qkv, L1_attn_w_out, L1_attn_b_out), axis=-1)
    x = _layernorm(x + _L1_xattn_ref(x, ctx_1024, mask_BxS2_bk0, L1_xattn_Wq, L1_xattn_bq, L1_xattn_Wkv, L1_xattn_bkv, L1_xattn_qn_w, L1_xattn_qn_b, L1_xattn_kn_w, L1_xattn_kn_b, L1_xattn_Wo, L1_xattn_bo), axis=-1)
    x = _layernorm(x + _L1_ffn_ref(x, L1_ffn_Wg, L1_ffn_W1, L1_ffn_W2), axis=-1)
    return x

_drawn_inputs = setup_inputs


def setup_inputs(seed=0):
    import zlib

    import numpy as np

    out = dict(_drawn_inputs(seed))
    spreads = {'L0_attn_ln_gamma': (1.0, 0.6),
     'L0_attn_ln_beta': (0.0, 0.1),
     'L0_xattn_bq': (0.0, 0.336),
     'L0_xattn_bk': (0.0, 0.8),
     'L0_xattn_bv': (0.0, 0.1),
     'L0_xattn_bo': (0.0, 0.1),
     'L1_xattn_bq': (0.0, 0.8),
     'L1_xattn_bkv': (0.0, 0.1),
     'L1_xattn_qn_w': (1.0, 0.6),
     'L1_xattn_qn_b': (0.0, 0.8),
     'L1_xattn_kn_w': (1.0, 0.6),
     'L1_xattn_kn_b': (0.0, 0.8),
     'L1_xattn_bo': (0.0, 0.1)}
    factors = {'L0_attn_rel': 2.783,
     'L1_attn_b_qkv': 5.27,
     'L1_attn_b_out': 6.236,
     'L1_xattn_Wq': 3.213,
     'L1_ffn_Wg': 3.558,
     'L1_ffn_W1': 3.413,
     'L1_ffn_W2': 3.341}
    for name, (base, spread) in spreads.items():
        noise = np.random.default_rng([zlib.crc32(name.encode()), seed]).standard_normal(out[name].shape)
        drawn = base * np.exp(spread * noise) if base else spread * noise
        out[name] = jnp.asarray(drawn.astype(out[name].dtype))
    for name, factor in factors.items():
        out[name] = (out[name] * factor).astype(out[name].dtype)
    return out
```

```python
from contextlib import ExitStack

import concourse.bass as bass
from concourse import mybir
from concourse.alu_op_type import AluOpType as ALU

FP32 = mybir.dt.float32
BF16 = mybir.dt.bfloat16
INT32 = mybir.dt.int32
UINT8 = mybir.dt.uint8
ACT = mybir.ActivationFunctionType
AX = mybir.AxisListType

P = 128
T = 2048
D = 256
FT = D // P
NT = T // P
TC = 1601
CT = -(-TC // P)
H = 16
DH = D // H
BANK = 512
CHUNK = 1024
PARTS = 3
PAIRS = 6 * DH
NEG = -1.0e20
MAXREL = 128
LN_EPS = 1e-5
QN_EPS = 1e-6


def cols_of(n, size=BANK):
    return [(c, min(c + size, n)) for c in range(0, n, size)]


class Mem:

    retired = []

    def __init__(self, nc, stack, tag):
        self.nc, self.stack, self.tag, self.sems = nc, stack, tag, []
        stack.callback(self.give_back)

    def give_back(self):
        Mem.retired += self.sems

    @staticmethod
    def reclaim(nc):
        nc.clear_and_free_semaphores(list(Mem.retired))
        nc.all_engine_barrier()
        Mem.retired.clear()

    def sb(self, name, shape, dtype=FP32):
        return self.stack.enter_context(self.nc.sbuf_tensor(f"{self.tag}_{name}", shape, dtype))

    def ps(self, name, shape, dtype=FP32):
        return self.stack.enter_context(self.nc.psum_tensor(f"{self.tag}_{name}", shape, dtype))

    def sem(self, name):
        self.sems.append(self.nc.alloc_semaphore(f"{self.tag}_{name}"))
        return self.sems[-1]




def to_feature_major(nc, tag, x_tok, x_fm, ident, scale=None, shift=None):
    with ExitStack() as st:
        m = Mem(nc, st, tag)
        ps = [m.ps(f"ps{b}", [P, BANK]) for b in range(2)]
        turned = m.sem("turned")
        kept = m.sem("kept")
        groups = [(f, g) for f in range(FT) for g in range(NT // 4)]
        with nc.Block() as block:

            @block.tensor
            def _(pe):
                for n, (f, g) in enumerate(groups):
                    if n >= 2:
                        pe.wait_ge(kept, n - 1)
                    for j in range(4):
                        last = pe.transpose(ps[n % 2][:, j * P:(j + 1) * P],
                                            x_tok[:, 4 * g + j, f * P:(f + 1) * P], ident[:, :])
                    last.then_inc(turned, 1)

            @block.scalar
            def _(act):
                for n, (f, g) in enumerate(groups):
                    act.wait_ge(turned, n + 1)
                    dst = x_fm[:, f, g * BANK:(g + 1) * BANK]
                    if scale is None:
                        act.activation(dst, ps[n % 2][:, :], ACT.Copy).then_inc(kept, 1)
                    else:
                        act.activation(dst, ps[n % 2][:, :], ACT.Identity, bias=shift[:, f:f + 1],
                                       scale=scale[:, f:f + 1]).then_inc(kept, 1)




def project_split(nc, tag, jobs, v_job, scan=None):
    R = 4
    with ExitStack() as st:
        m = Mem(nc, st, tag)
        ps = [m.ps(f"ps{b}", [P, BANK]) for b in range(R)]
        pv = [m.ps(f"pv{b}", [P, BANK]) for b in range(2)]
        whole = [m.sb(f"whole{b}", [P, BANK]) for b in range(2)]
        rest = [m.sb(f"rest{b}", [P, BANK]) for b in range(R)]
        parts = [m.sb(f"parts{b}", [P, PARTS, BANK], BF16) for b in range(R)]
        done = m.sem("done")
        cast = m.sem("cast")
        resid = m.sem("resid")
        second = m.sem("second")
        third = m.sem("third")
        stored = [m.sem(f"stored{b}") for b in range(R)]
        vdone = m.sem("vdone")
        vkept = m.sem("vkept")
        scanned = m.sem("scanned")
        work = [(j, f, lo, hi) for j in jobs for f in range(FT) for lo, hi in cols_of(j[2])]
        vw, vsrc, vtok, vbias, vdst = v_job
        vtiles = [(n, min(P, vtok - n * P)) for n in range(-(-vtok // P))]

        def v_tile(pe, n):
            t, rows = vtiles[n]
            if n >= 2:
                pe.wait_ge(vkept, n - 1)
            for k in range(FT):
                last = pe.matmul(pv[n % 2][0:rows, 0:D], vsrc[:, k, t * P:t * P + rows],
                                 vw[:, k, :], start=(k == 0), stop=(k == FT - 1))
            last.then_inc(vdone, 1)

        def v_out(dve, n):
            t, rows = vtiles[n]
            dve.wait_ge(vdone, n + 1)
            dve.tensor_tensor(vdst[0:rows, t, :], pv[n % 2][0:rows, 0:D], vbias[0:rows, :],
                              ALU.add).then_inc(vkept, 1)

        with nc.Block() as block:

            @block.tensor
            def _(pe):
                for n, (j, f, lo, hi) in enumerate(work):
                    if j[0] is not None:
                        if n >= R:
                            pe.wait_ge(cast, n - R + 1)
                        for k in range(FT):
                            last = pe.matmul(ps[n % R][:, 0:hi - lo], j[0][:, k, f * P:(f + 1) * P],
                                             j[1][:, k, lo:hi], start=(k == 0), stop=(k == FT - 1))
                        last.then_inc(done, 1)
                    if n < len(vtiles):
                        v_tile(pe, n)
                for n in range(len(work), len(vtiles)):
                    v_tile(pe, n)

            @block.scalar
            def _(act):
                def tail(n):
                    _, _, lo, hi = work[n]
                    act.wait_ge(resid, n + 1)
                    act.activation(parts[n % R][:, 1, 0:hi - lo], rest[n % R][:, 0:hi - lo],
                                   ACT.Copy).then_inc(second, 1)

                for n, (j, f, lo, hi) in enumerate(work):
                    w = hi - lo
                    if j[0] is None:
                        src = j[1][:, f, lo:hi]
                    else:
                        act.wait_ge(done, n + 1)
                        src = ps[n % R][:, 0:w]
                    if n >= R:
                        act.wait_ge(stored[n % R], 16 * PARTS * (n // R))
                    if n >= 2:
                        act.wait_ge(resid, n - 1)
                    act.activation(whole[n % 2][:, 0:w], src, ACT.Identity,
                                   bias=j[4][:, f:f + 1], scale=j[3])
                    act.activation(parts[n % R][:, 0, 0:w], src, ACT.Identity,
                                   bias=j[4][:, f:f + 1], scale=j[3]).then_inc(cast, 1)
                    if n >= 1:
                        tail(n - 1)
                tail(len(work) - 1)

            @block.vector
            def _(dve):
                for n, (j, f, lo, hi) in enumerate(work):
                    w = hi - lo
                    dve.wait_ge(cast, n + 1)
                    if n >= R:
                        dve.wait_ge(third, n - R + 1)
                        dve.wait_ge(second, n - R + 1)
                    dve.tensor_tensor(rest[n % R][:, 0:w], whole[n % 2][:, 0:w],
                                      parts[n % R][:, 0, 0:w], ALU.subtract).then_inc(resid, 1)
                    if n < len(vtiles):
                        v_out(dve, n)
                for n in range(len(work), len(vtiles)):
                    v_out(dve, n)
                if scan is not None:
                    rows_sb, groups, largest = scan
                    for t in range(NT):
                        dve.wait_ge(groups[t * len(groups) // NT], 16)
                        dve.tensor_reduce(largest[:, t:t + 1], rows_sb[:, t, :], op=ALU.max, axis=AX.X,
                                          apply_absolute_value=True).then_inc(scanned, 1)

            @block.gpsimd
            def _(pool):
                for n, (j, f, lo, hi) in enumerate(work):
                    w = hi - lo
                    pool.wait_ge(second, n + 1)
                    pool.tensor_tensor(parts[n % R][:, 2, 0:w], rest[n % R][:, 0:w],
                                       parts[n % R][:, 1, 0:w], ALU.subtract).then_inc(third, 1)

            @block.sync
            def _(sp):
                for n, (j, f, lo, hi) in enumerate(work):
                    sp.wait_ge(third, n + 1)
                    for t in range(PARTS):
                        at = PARTS - 1 - t if j[6] else t
                        sp.dma_start(j[5][f * P:(f + 1) * P, at, lo:hi],
                                     parts[n % R][:, t, 0:hi - lo]).then_inc(stored[n % R], 16)
                for b in range(R):
                    sp.wait_ge(stored[b], 16 * PARTS * len(work[b::R]))




def attention(nc, tag, nk, mode, q_dram, k_dram, v_sb, o_tok, ident, flip=None, bands=None,
              band_dram=None, key_row=None, mask_sb=None, mask_flag=None, neg_eye=None, ident_bf=None):
    causal = mode in ("rel", "tri")
    KT = -(-nk // P)
    rows_m = PAIRS + (mode == "row")
    rows_e = rows_m + PARTS
    loads = 8 + (mode == "rel")

    def rows_of(kt):
        return min(P, nk - kt * P)

    def first_q(kt):
        return kt * P if causal else 0

    def chunks(kt):
        return [(max(lo, first_q(kt)), hi) for lo, hi in cols_of(T, CHUNK) if hi > first_q(kt)]

    STEPS = [(kt, c) for kt in range(KT) for c in chunks(kt)]
    NC = len(STEPS)
    FIRST_OF = [min(n for n, s in enumerate(STEPS) if s[0] == kt) for kt in range(KT)] + [NC]
    UNITS = [(i, c, lo, hi) for i in range(NT)
             for c, (lo, hi) in enumerate(cols_of((i + 1) * P if causal else nk))]
    NU = len(UNITS)
    SWITCH = 5 if causal else 9
    TURN = SWITCH + 2
    weight = [T - first_q(kt) for kt in range(KT)]
    split = NU - int(round(NU * sum(weight[:SWITCH]) / sum(weight)))

    def shared_out(units, steps):
        total, given, at, out = sum(weight[s] for s in steps), 0, 0, {}
        for s in steps:
            given += weight[s]
            end = round(len(units) * given / total)
            out[s] = units[at:end]
            at = end
        return out

    LATE = shared_out(list(range(split, NU)), range(SWITCH))
    EARLY = shared_out(list(range(split)), range(SWITCH, KT))

    def plan(k):
        events = []
        for kt in range(KT):
            todo = []
            if kt < SWITCH and k + 1 < H:
                todo = [("unit", 1, u) for u in LATE[kt]]
            if kt >= SWITCH and k + 2 < H:
                todo = [("unit", 2, u) for u in EARLY[kt]]

            def some(turns_left):
                n = -(-len(todo) // turns_left)
                events.extend(todo[:n])
                del todo[:n]

            chunks_here = range(FIRST_OF[kt], FIRST_OF[kt + 1])
            for n in chunks_here:
                events.append(("score", n))
                some(chunks_here[-1] - n + 2)
            if kt > 0:
                events.append(("v", 0, kt - 1))
            elif k > 0:
                events.append(("v", 1, KT - 1))
            some(1)
            if kt == 2 and k > 0:
                events.append(("out", 1))
            if kt == TURN and k + 1 < H:
                events.append(("max", 1))
        return events

    RING = 3
    PER_HEAD = NU + 2
    assert PER_HEAD % RING == 0 and NC % 2 == 0

    def is_slot(event):
        return event[0] in ("unit", "out", "max")

    START = [NU + split + 1]
    for k in range(H):
        START.append(START[-1] + sum(map(is_slot, plan(k))))
    assert all(START[k] == START[1] + (k - 1) * PER_HEAD for k in range(1, H - 1))

    def start_of(h):
        return START[h] if isinstance(h, int) else (h - 1) * PER_HEAD + START[1]

    def maxima_end(h):
        if isinstance(h, int) and h == 0:
            return NU
        k = h - 1 if isinstance(h, int) else 4
        slots = [e for e in plan(k) if is_slot(e)]
        return start_of(h - 1) + max(n for n, e in enumerate(slots) if e[:2] == ("unit", 1)) + 1

    def out_turned(h):
        k = h + 1 if isinstance(h, int) else 4
        slots = [e for e in plan(k) if is_slot(e)]
        return start_of(h + 1) + slots.index(("out", 1)) + 1

    with ExitStack() as st:
        m = Mem(nc, st, tag)
        q_exp = [m.sb(f"q_exp{b}", [P, T], BF16) for b in range(2)]
        k_exp = [m.sb(f"k_exp{b}", [P, nk], BF16) for b in range(2)]
        q_max = [m.sb(f"q_max{b}", [P, T], BF16) for b in range(2)]
        k_max = [m.sb(f"k_max{b}", [P, nk], BF16) for b in range(2)]
        probs = [m.sb(f"probs{b}", [P, T]) for b in range(2)]
        v_head = [m.sb(f"v_head{b}", [P, KT, 32]) for b in range(2)]
        o_sb = m.sb("o_sb", [P, BANK])
        max_part = m.sb("max_part", [P, NT, 4])
        max_neg = m.sb("max_neg", [P, NT])
        max_rest = m.sb("max_rest", [P, NT])
        max_bf = m.sb("max_bf", [P, P], BF16)
        max_row = m.sb("max_row", [PARTS * NT, P], BF16)
        denom = m.sb("denom", [P, NT])
        if mode == "rel":
            band_e = [m.sb(f"band_e{b}", [P, PARTS, 2 * P], BF16) for b in range(2)]
            band_m = [m.sb(f"band_m{b}", [P, PARTS, 2 * P], BF16) for b in range(2)]
        scores = [m.ps(f"scores{b}", [P, CHUNK]) for b in range(2)]
        ring = [m.ps(f"ring{b}", [P, BANK]) for b in range(RING)]
        o_ps = m.ps("o_ps", [P, BANK])

        head_in = [m.sem(f"head_in{b}") for b in range(2)]
        max_in = [m.sem(f"max_in{b}") for b in range(2)]
        row_in = [m.sem(f"row_in{b}") for b in range(2)]
        consts = m.sem("consts")
        key_in = m.sem("key_in")
        v_set = m.sem("v_set")
        passed = m.sem("passed")
        v_tail = m.sem("v_tail")
        v_in = m.sem("v_in")
        scored = m.sem("scored")
        expd = m.sem("expd")
        pv_done = m.sem("pv_done")
        filled = m.sem("filled")
        emptied = m.sem("emptied")
        neg_done = m.sem("neg_done")
        cut = m.sem("cut")
        row_sb = m.sem("row_sb")
        o_kept = m.sem("o_kept")
        denoms = m.sem("denoms")

        n_consts = 3 + 4 * (mode == "row")

        def at_least(eng, sem, value):
            if not (isinstance(value, int) and value <= 0):
                eng.wait_ge(sem, value)

        def per_head(body):
            def program(eng, looped=H // 2 - 1):
                for h in (0, 1):
                    body(eng, h, 0, h)
                with eng.Fori(1, looped) as pair:
                    for b in range(2):
                        body(eng, 2 * pair + b, pair, b)
                for h in range(2 * looped, H):
                    body(eng, h, h // 2, h % 2)
            return program

        def known(h):
            return h if isinstance(h, int) else 4

        with nc.Block() as block:

            @block.sync
            def _(sp):
                def operands(q, k, sem, h):
                    for dst, src, order in ((q, q_dram, (0, 1, 0)), (k, k_dram, (1, 2, 2))):
                        head = src[bass.ds(h * DH, DH), :, :]
                        sp.dma_start(dst[0:3 * DH, :], head.rearrange("d t n -> (d t) n")).then_inc(sem, 16)
                        for n, t in enumerate(order):
                            sp.dma_start(dst[(3 + n) * DH:(4 + n) * DH, :], head[:, t, :]).then_inc(sem, 16)

                def load_exp(h, b):
                    at_least(sp, scored, (h - 1) * NC)
                    operands(q_exp[b], k_exp[b], head_in[b], h)
                    if mode == "rel":
                        sp.dma_start(band_e[b][:, :, :], band_dram(h, 0)).then_inc(head_in[b], 16)

                def load_max(h, b):
                    if known(h) >= 2:
                        sp.wait_ge(filled, maxima_end(h - 2))
                    operands(q_max[b], k_max[b], max_in[b], h)
                    if mode == "rel":
                        sp.dma_start(band_m[b][:, :, :], band_dram(h, 1)).then_inc(max_in[b], 16)

                def load_row(h, b):
                    sp.wait_ge(row_sb, h + 1)
                    for t in range(PARTS):
                        sp.dma_start(q_exp[b][rows_m + t:rows_m + t + 1, :].rearrange("o (i q) -> o i q", i=NT),
                                     max_row[t * NT:(t + 1) * NT, :]).then_inc(row_in[b], 16)

                if mode == "row":
                    sp.wait_ge(consts, n_consts)
                    for k in k_max + k_exp:
                        sp.dma_start(k[PAIRS:PAIRS + 1, :], key_row).then_inc(key_in, 16)
                load_max(0, 0)
                load_max(1, 1)
                load_exp(0, 0)
                load_row(0, 0)
                load_max(2, 0)

                def body(sp, h, pair, b):
                    k = known(h)
                    if k + 1 < H:
                        load_exp(h + 1, 1 - b)
                        load_row(h + 1, 1 - b)
                    if k + 3 < H:
                        load_max(h + 3, 1 - b)
                per_head(body)(sp, H // 2 - 2)

            @block.tensor
            def _(pe):
                pe.wait_ge(consts, n_consts)
                if mode == "row":
                    pe.wait_ge(key_in, 64)

                def unit(u, slot, bank, b, nth, general):
                    i, c, lo, hi = UNITS[u]
                    if u == 0:
                        pe.wait_ge(max_in[b], 16 * loads * (nth + 1))
                    at_least(pe, emptied, slot - RING + 1)
                    adds = []
                    if mode == "rel":
                        for x in (i - 1, i):
                            if x >= 0 and lo <= x * P < hi:
                                for t in range(PARTS):
                                    adds.append((bank[:, x * P - lo:(x + 1) * P - lo], flip[:, :],
                                                 band_m[b][:, t, (x - i + 1) * P:(x - i + 2) * P]))
                    if mode == "tri" and hi == (i + 1) * P:
                        adds.append((bank[:, i * P - lo:(i + 1) * P - lo], flip[:, :], bands[:, 1, :]))
                    if general:
                        adds.append((bank[:, 0:hi - lo], neg_eye[:, :], mask_sb[:, i, lo:hi]))
                    last = pe.matmul(bank[:, 0:hi - lo], q_max[b][0:rows_m, i * P:(i + 1) * P],
                                     k_max[b][0:rows_m, lo:hi], start=True, stop=True)
                    for out, lhs, rhs in adds:
                        last = pe.matmul(out, lhs, rhs, start=False, stop=True, skip_group_check=True)
                    last.then_inc(filled, 1)

                def score(kt, n, h, b, general):
                    lo, hi = STEPS[n][1]
                    bank = scores[n % 2]
                    base = lo // CHUNK * CHUNK
                    rows = rows_of(kt)
                    at_least(pe, expd, h * NC + n - 1)
                    pieces = [(max(lo, s), min(hi, s + BANK)) for s in range(base, base + CHUNK, BANK)
                              if min(hi, s + BANK) > max(lo, s)]
                    for s, e in pieces:
                        adds = []
                        if mode == "rel":
                            for x in (kt, kt + 1):
                                if s <= x * P < e:
                                    for t in range(PARTS):
                                        adds.append((x * P, flip[:, :], band_e[b][:, t, (x - kt) * P:(x - kt + 1) * P]))
                        if mode == "tri" and s == kt * P:
                            adds.append((s, flip[:, :], bands[:, 0, :]))
                        if general:
                            for x in range(s // P, e // P):
                                adds.append((x * P, mask_sb[:, x, kt * P:kt * P + rows], neg_eye[:, :]))
                        last = pe.matmul(bank[0:rows, s - base:e - base],
                                         k_exp[b][0:rows_e, kt * P:kt * P + rows],
                                         q_exp[b][0:rows_e, s:e], start=True, stop=True)
                        for a, (x, lhs, rhs) in enumerate(adds):
                            last = pe.matmul(bank[0:rows, x - base:x - base + P], lhs, rhs, start=False,
                                             stop=True, skip_group_check=True)
                    last.then_inc(scored, 1)

                def times_v(kt, h, b):
                    rows = rows_of(kt)
                    pe.wait_ge(expd, h * NC + FIRST_OF[kt + 1])
                    if kt == 0:
                        pe.wait_ge(v_in, h + 1)
                        at_least(pe, o_kept, h)
                    i0 = kt if causal else 0
                    tile = probs[(b * KT + kt) % 2]
                    for j in range(4):
                        c0 = -(-(i0 - j) // 4) if i0 > j else 0
                        if c0 >= 4:
                            continue
                        last_kt = max(k for k in range(KT) if not causal or k <= 12 + j)
                        src = tile[0:rows, :].rearrange("k (c j q) -> k c j q", c=4, j=4)[:, c0:4, j, :]
                        mm = pe.matmul(o_ps[32 * j:32 * j + 32, c0 * P:BANK], v_head[b][0:rows, kt, :], src,
                                       start=kt == 0, stop=kt == last_kt, tile_position=(0, 32 * j))
                    mm.then_inc(pv_done, 1)

                def turn_max(h, slot, bank):
                    pe.wait_ge(cut, 4 * (h + 1))
                    at_least(pe, emptied, slot - RING + 1)
                    pe.transpose(bank[:, 0:P // 2].bitcast(BF16), max_bf[:, :],
                                 ident_bf[:, :]).then_inc(filled, 1)

                def turn_out(h, slot, bank):
                    pe.wait_ge(o_kept, h + 1)
                    at_least(pe, emptied, slot - RING + 1)
                    for c in range(4):
                        last = pe.transpose(bank[:, c * P:(c + 1) * P], o_sb[:, c * P:(c + 1) * P], ident[:, :])
                    last.then_inc(filled, 1)

                def everything(general):
                    for slot in range(NU + split):
                        u, g = (slot, 0) if slot < NU else (slot - NU, 1)
                        unit(u, slot, ring[slot % RING], g, 0, general)
                    turn_max(0, NU + split, ring[(NU + split) % RING])

                    def steps(_, h, pair, b):
                        pe.wait_ge(head_in[b], 16 * loads * (pair + 1))
                        pe.wait_ge(row_in[b], 16 * PARTS * (pair + 1))
                        slot, place = start_of(h), START[known(h)]
                        for event in plan(known(h)):
                            if event[0] == "score":
                                score(STEPS[event[1]][0], event[1], h, b, general)
                            elif event[0] == "v":
                                times_v(event[2], h - event[1], (b + event[1]) % 2)
                            else:
                                bank = ring[place % RING]
                                if event[0] == "unit":
                                    ahead = event[1]
                                    unit(event[2], slot, bank, (b + ahead) % 2, pair + (b + ahead) // 2, general)
                                elif event[0] == "out":
                                    turn_out(h - 1, slot, bank)
                                else:
                                    turn_max(h + 1, slot, bank)
                                slot, place = slot + 1, place + 1

                    per_head(steps)(pe)
                    times_v(KT - 1, H - 1, 1)
                    turn_out(H - 1, START[H], ring[START[H] % RING])

                if mode == "mask":
                    flag = pe.value_load(mask_flag, min_val=0, max_val=1)
                    with pe.If(flag == 0):
                        everything(False)
                    with pe.Else():
                        everything(True)
                else:
                    everything(False)

            @block.scalar
            def _(act):
                def keep_out(h):
                    act.wait_ge(pv_done, (h + 1) * KT)
                    if known(h) > 0:
                        act.wait_ge(filled, out_turned(h - 1))
                    act.activation(o_sb[:, :], o_ps[:, :], ACT.Copy).then_inc(o_kept, 1)

                def body(act, h, pair, b):
                    k = known(h)
                    for kt in range(KT):
                        rows = rows_of(kt)
                        for n in range(FIRST_OF[kt], FIRST_OF[kt + 1]):
                            lo, hi = STEPS[n][1]
                            base = lo // CHUNK * CHUNK
                            act.wait_ge(scored, h * NC + n + 1)
                            if n == FIRST_OF[kt]:
                                at_least(act, pv_done, h * KT + kt - 1)
                            act.activation(probs[(b * KT + kt) % 2][0:rows, lo:hi],
                                           scores[n % 2][0:rows, lo - base:hi - base],
                                           ACT.Exp).then_inc(expd, 1)
                        if kt == 0 and k > 0:
                            keep_out(h - 1)

                per_head(body)(act)
                keep_out(H - 1)

            @block.vector
            def _(dve):
                dve.memset(max_part[:, :, :], -3.0e38).then_inc(consts, 1)
                for k in k_exp:
                    dve.memset(k[PAIRS:rows_e, :], 1.0).then_inc(consts, 1)
                if mode == "row":
                    for q in q_exp + q_max:
                        dve.memset(q[PAIRS:PAIRS + 1, :], 1.0).then_inc(consts, 1)
                dve.wait_ge(consts, n_consts)

                def take(u, h, slot, bank):
                    i, c, lo, hi = UNITS[u]
                    if u == 0:
                        at_least(dve, neg_done, h)
                    dve.wait_ge(filled, slot + 1)
                    dve.tensor_reduce(max_part[:, i, c:c + 1], bank[:, 0:hi - lo], op=ALU.max,
                                      axis=AX.X).then_inc(emptied, 1)
                    if u == NU - 1:
                        dve.wait_ge(emptied, slot + 1)
                        at_least(dve, cut, 4 * h)
                        dve.tensor_reduce(max_neg[:, :], max_part[:, :, :], op=ALU.max, axis=AX.X,
                                          negate=True).then_inc(neg_done, 1)

                def keep_row(h, pair, b, slot, bank):
                    dve.wait_ge(filled, slot + 1)
                    if pair is not None:
                        dve.wait_ge(row_in[b], 16 * PARTS * (pair + 1))
                    dve.tensor_copy(max_row[:, :], bank[0:PARTS * NT, 0:P // 2].bitcast(BF16))\
                        .then_inc(row_sb, 1)
                    dve.wait_ge(row_sb, h + 1)
                    dve.sem_inc(emptied, 1)

                def normalise(h, slot, bank):
                    dve.wait_ge(filled, slot + 1)
                    turned_o = bank[:, :].rearrange("q (i c) -> q i c", i=NT)
                    dve.reciprocal(denom[:, :], turned_o[:, :, DH]).then_inc(denoms, 1)
                    dve.wait_ge(denoms, h + 1)
                    dve.tensor_tensor(o_tok[:, :, bass.ds(h * DH, DH)], turned_o[:, :, 0:DH],
                                      denom[:, :].unsqueeze(2).broadcast_to([P, NT, DH]),
                                      ALU.mult).then_inc(emptied, 1)

                for slot in range(NU + split):
                    u, g = (slot, 0) if slot < NU else (slot - NU, 1)
                    take(u, g, slot, ring[slot % RING])
                keep_row(0, None, 0, NU + split, ring[(NU + split) % RING])

                def body(dve, h, pair, b):
                    slot, place = start_of(h), START[known(h)]
                    for event in filter(is_slot, plan(known(h))):
                        bank = ring[place % RING]
                        if event[0] == "unit":
                            take(event[2], h + event[1], slot, bank)
                        elif event[0] == "out":
                            normalise(h - 1, slot, bank)
                        else:
                            keep_row(h + 1, pair, b, slot, bank)
                        slot, place = slot + 1, place + 1

                per_head(body)(dve)
                dve.wait_ge(emptied, START[H])
                normalise(H - 1, START[H], ring[START[H] % RING])

            @block.gpsimd
            def _(pool):
                for b in range(2):
                    pool.memset(v_head[b][:, :, :], 0.0).then_inc(v_set, 1)
                pool.wait_ge(v_set, 2)
                for b in range(2):
                    pool.memset(v_head[b][:, :, DH:DH + 1], 1.0).then_inc(v_set, 1)
                pool.memset(max_bf[:, :], 0.0).then_inc(v_set, 1)
                pool.wait_ge(v_set, 5)

                def copy_v(h, b):
                    at_least(pool, pv_done, (h - 1) * KT)
                    pool.sem_inc(passed, 1)
                    full = nk // P
                    if full < KT:
                        pool.tensor_copy(v_head[b][0:nk - full * P, full, 0:DH],
                                         v_sb[0:nk - full * P, full, bass.ds(h * DH, DH)]).then_inc(v_tail, 1)
                        pool.wait_ge(v_tail, h + 1)
                        pool.sem_inc(passed, 1)
                    pool.tensor_copy(v_head[b][:, 0:full, 0:DH],
                                     v_sb[:, 0:full, bass.ds(h * DH, DH)]).then_inc(v_in, 1)

                def split_max(h):
                    pool.wait_ge(neg_done, h + 1)
                    at_least(pool, row_sb, h)
                    pool.sem_inc(passed, 1)
                    pool.tensor_copy(max_bf[:, 0:NT], max_neg[:, :]).then_inc(cut, 1)
                    pool.wait_ge(cut, 4 * h + 1)
                    pool.tensor_tensor(max_rest[:, :], max_neg[:, :], max_bf[:, 0:NT],
                                       ALU.subtract).then_inc(cut, 1)
                    pool.wait_ge(cut, 4 * h + 2)
                    pool.sem_inc(passed, 1)
                    pool.tensor_copy(max_bf[:, NT:2 * NT], max_rest[:, :]).then_inc(cut, 1)
                    pool.wait_ge(cut, 4 * h + 3)
                    pool.tensor_tensor(max_bf[:, 2 * NT:3 * NT], max_rest[:, :], max_bf[:, NT:2 * NT],
                                       ALU.subtract).then_inc(cut, 1)

                copy_v(0, 0)
                split_max(0)

                def body(pool, h, pair, b):
                    if known(h) + 1 < H:
                        copy_v(h + 1, 1 - b)
                        split_max(h + 1)

                per_head(body)(pool)




def project_norm(nc, tag, x_tok, src_fm=None, w=None, bias=None, ones=None, resid=1.0, eps=LN_EPS,
                 out=None, addend=None):
    out = x_tok if out is None else out
    KF = 0 if src_fm is None else src_fm.shape[1]
    with ExitStack() as st:
        m = Mem(nc, st, tag)
        ps = [m.ps(f"ps{b}", [P, BANK]) for b in range(2)] if KF else None
        y = m.sb("y", [P, NT, D])
        stats = m.sb("stats", [P, NT, 6])
        mean_var = m.sb("mean_var", [P, NT, 2])
        dev = m.sb("dev", [P, NT])
        rstd = m.sb("rstd", [P, NT])
        made = m.sem("made")
        summed = m.sem("summed")
        counted = m.sem("counted")
        ready = m.sem("ready")
        shifted = m.sem("shifted")
        rooted = m.sem("rooted")
        inverted = m.sem("inverted")
        normed = m.sem("normed")
        with nc.Block() as block:
            if KF:
                @block.tensor
                def _(pe):
                    for t in range(NT):
                        if t >= 2:
                            pe.wait_ge(summed, t - 1)
                        for k in range(KF):
                            last = pe.matmul(ps[t % 2][:, 0:D], src_fm[:, k, t * P:(t + 1) * P], w[:, k, :],
                                             start=k == 0, stop=k == KF - 1 and bias is None)
                        if bias is not None:
                            last = pe.matmul(ps[t % 2][:, 0:D], ones[0:1, :], bias[0:1, :],
                                             start=False, stop=True)
                        last.then_inc(made, 1)

            @block.vector
            def _(dve):
                src = y if KF or addend is not None else x_tok
                for t in range(NT):
                    if KF:
                        dve.wait_ge(made, t + 1)
                        dve.scalar_tensor_tensor(out=y[:, t, :], in0=x_tok[:, t, :], scalar=resid,
                                                 in1=ps[t % 2][:, 0:D], op0=ALU.mult,
                                                 op1=ALU.add).then_inc(summed, 1)
                        dve.wait_ge(summed, t + 1)
                    elif addend is not None:
                        dve.tensor_tensor(y[:, t, :], x_tok[:, t, :], addend[:, t, :],
                                          ALU.add).then_inc(summed, 1)
                        dve.wait_ge(summed, t + 1)
                    dve.bn_stats(stats[:, t, :], src[:, t, :]).then_inc(counted, 1)
                    dve.wait_ge(counted, t + 1)
                    dve.bn_aggr(mean_var[:, t, :], stats[:, t, :]).then_inc(ready, 1)
                dve.wait_ge(ready, NT)
                dve.tensor_scalar(dev[:, :], mean_var[:, :, 1], eps, None, ALU.add).then_inc(shifted, 1)
                dve.wait_ge(rooted, 1)
                dve.reciprocal(rstd[:, :], dev[:, :]).then_inc(inverted, 1)
                dve.wait_ge(inverted, 1)
                for t in range(NT):
                    dve.tensor_scalar(out[:, t, :], src[:, t, :], mean_var[:, t, 0:1], rstd[:, t:t + 1],
                                      ALU.subtract, ALU.mult).then_inc(normed, 1)

            @block.scalar
            def _(act):
                act.wait_ge(shifted, 1)
                act.activation(dev[:, :], dev[:, :], ACT.Sqrt).then_inc(rooted, 1)


def head_norm(nc, tag, jobs, group_mean, eps_cell):
    with ExitStack() as st:
        m = Mem(nc, st, tag)
        raw = m.ps("raw", [P, BANK])
        mean = m.ps("mean", [P, BANK])
        var = m.ps("var", [P, BANK])
        lin = m.sb("lin", [P, BANK])
        cen = m.sb("cen", [P, BANK])
        sq = m.sb("sq", [P, BANK])
        dev = m.sb("dev", [P, BANK])
        inv = m.sb("inv", [P, BANK])
        s_raw, s_lin, s_mean, s_cen, s_sq, s_var, s_dev, s_inv, s_scaled, s_out = (
            m.sem(n) for n in ("raw_done", "lin_done", "mean_done", "centred", "squared", "var_done",
                               "rooted", "inverted", "scaled", "affine"))
        work = [(j, f, lo, hi) for j in jobs for f in range(FT) for lo, hi in cols_of(j[2])]
        with nc.Block() as block:

            @block.tensor
            def _(pe):
                for n, (j, f, lo, hi) in enumerate(work):
                    w = hi - lo
                    if n:
                        pe.wait_ge(s_lin, n)
                    for k in range(FT):
                        last = pe.matmul(raw[:, 0:w], j[0][:, k, f * P:(f + 1) * P], j[1][:, k, lo:hi],
                                         start=k == 0, stop=k == FT - 1)
                    last.then_inc(s_raw, 1)
                    pe.wait_ge(s_lin, n + 1)
                    if n:
                        pe.wait_ge(s_cen, n)
                    pe.matmul(mean[:, 0:w], group_mean[:, :], lin[:, 0:w], start=True,
                              stop=True).then_inc(s_mean, 1)
                    pe.wait_ge(s_sq, n + 1)
                    if n:
                        pe.wait_ge(s_dev, n)
                    pe.matmul(var[:, 0:w], group_mean[:, :], sq[:, 0:w], start=True,
                              stop=True).then_inc(s_var, 1)

            @block.scalar
            def _(act):
                for n, (j, f, lo, hi) in enumerate(work):
                    w = hi - lo
                    act.wait_ge(s_raw, n + 1)
                    if n:
                        act.wait_ge(s_cen, n)
                    act.activation(lin[:, 0:w], raw[:, 0:w], ACT.Identity, bias=j[3][:, f:f + 1],
                                   scale=1.0).then_inc(s_lin, 1)
                    act.wait_ge(s_cen, n + 1)
                    if n:
                        act.wait_ge(s_var, n)
                    act.activation(sq[:, 0:w], cen[:, 0:w], ACT.Square).then_inc(s_sq, 1)
                    act.wait_ge(s_var, n + 1)
                    if n:
                        act.wait_ge(s_inv, n)
                    act.activation(dev[:, 0:w], var[:, 0:w], ACT.Sqrt, bias=eps_cell[:, 0:1],
                                   scale=1.0).then_inc(s_dev, 1)

            @block.vector
            def _(dve):
                for n, (j, f, lo, hi) in enumerate(work):
                    w = hi - lo
                    dve.wait_ge(s_mean, n + 1)
                    if n:
                        dve.wait_ge(s_scaled, n)
                        dve.wait_ge(s_sq, n)
                    dve.tensor_tensor(cen[:, 0:w], lin[:, 0:w], mean[:, 0:w], ALU.subtract).then_inc(s_cen, 1)
                    dve.wait_ge(s_dev, n + 1)
                    dve.reciprocal(inv[:, 0:w], dev[:, 0:w]).then_inc(s_inv, 1)
                    dve.wait_ge(s_inv, n + 1)
                    dst = j[6][:, f, lo:hi]
                    dve.tensor_tensor(dst, cen[:, 0:w], inv[:, 0:w], ALU.mult).then_inc(s_scaled, 1)
                    dve.wait_ge(s_scaled, n + 1)
                    dve.tensor_scalar(dst, dst, j[4][:, 0:1], j[5][:, 0:1], ALU.mult, ALU.add).then_inc(s_out, 1)



MAGIC = 12582912.0
QA = 32767.0
QW = 7.0
BLK = 32
F0 = 768
F0T = F0 // P


def dequantise(nc, tag, raw, fm, ident, O, I):
    OT, IT, NB = O // P, I // P, I // BLK
    with ExitStack() as st:
        m = Mem(nc, st, tag)
        scale = m.sb("scale", [P, OT * NB])
        inv = m.sb("inv", [P, OT * NB])
        q = m.sb("q", [P, OT * NB, BLK])
        ps = [m.ps(f"ps{b}", [P, BANK]) for b in range(2)]
        step = m.sem("step")
        turned = m.sem("turned")
        kept = m.sem("kept")
        w = raw.rearrange("p o (b i) -> p (o b) i", i=BLK)
        groups = [(o, i) for i in range(IT) for o in range(OT)]
        with nc.Block() as block:

            @block.vector
            def _(dve):
                def wide(t):
                    return t[:, :].unsqueeze(2).broadcast_to([P, OT * NB, BLK])

                dve.tensor_reduce(scale[:, :], w, op=ALU.max, axis=AX.X,
                                  apply_absolute_value=True).then_inc(step, 1)
                dve.wait_ge(step, 1)
                dve.tensor_scalar(scale[:, :], scale[:, :], 1.0 / QW, 1e-12, ALU.mult, ALU.max).then_inc(step, 1)
                dve.wait_ge(step, 2)
                dve.reciprocal(inv[:, :], scale[:, :]).then_inc(step, 1)
                dve.wait_ge(step, 3)
                dve.tensor_tensor(q[:, :, :], w, wide(inv), ALU.mult).then_inc(step, 1)
                dve.wait_ge(step, 4)
                dve.tensor_scalar(q[:, :, :], q[:, :, :], MAGIC, MAGIC, ALU.add, ALU.subtract).then_inc(step, 1)
                dve.wait_ge(step, 5)
                dve.tensor_scalar(q[:, :, :], q[:, :, :], -QW - 1.0, QW, ALU.max, ALU.min).then_inc(step, 1)
                dve.wait_ge(step, 6)
                dve.tensor_tensor(q[:, :, :], q[:, :, :], wide(scale), ALU.mult).then_inc(step, 1)

            @block.tensor
            def _(pe):
                pe.wait_ge(step, 7)
                flat = q[:, :, :].rearrange("p (o b) i -> p o (b i)", o=OT)
                for n, (o, i) in enumerate(groups):
                    if n >= 2:
                        pe.wait_ge(kept, n - 1)
                    pe.transpose(ps[n % 2][:, 0:P], flat[:, o, i * P:(i + 1) * P], ident[:, :]).then_inc(turned, 1)

            @block.scalar
            def _(act):
                for n, (o, i) in enumerate(groups):
                    act.wait_ge(turned, n + 1)
                    act.activation(fm[:, i, o * P:(o + 1) * P], ps[n % 2][:, 0:P], ACT.Copy).then_inc(kept, 1)


def quantised_ffn(nc, tag, x_tok, x_fm, wg, wu, gate, magic_cell):
    X, G, U, HID, O = range(5)
    RMAX = bass.bass_isa.ReduceOp.max
    with ExitStack() as st:
        m = Mem(nc, st, tag)
        up = m.sb("up", [P, F0T, T])
        sig = [m.sb(f"sig{b}", [P, T]) for b in range(2)]
        tmp = [m.sb(f"tmp{b}", [P, T]) for b in range(2)]
        part = m.sb("part", [P, 5, F0T])
        amax = m.sb("amax", [P, 5])
        wide = m.sb("wide", [P, 5])
        scale = m.sb("scale", [P, 5])
        inv = m.sb("inv", [P, 5])
        ps = [m.ps(f"ps{b}", [P, BANK]) for b in range(4)]
        made = m.sem("made")
        kept = m.sem("kept")
        seen = [m.sem(f"seen{n}") for n in range(5)]
        own = m.sem("own")
        all_max = m.sem("all_max")
        cells = m.sem("cells")
        added = [m.sem(f"added{n}") for n in range(5)]
        rounded = [m.sem(f"rounded{n}") for n in range(5)]
        sig_done = m.sem("sig_done")
        sig_added = m.sem("sig_added")
        sig_int = m.sem("sig_int")
        hid_done = m.sem("hid_done")
        o_done = m.sem("o_done")
        chunks = [(f, lo, hi) for f in range(F0T) for lo, hi in cols_of(T)]
        NCH = len(cols_of(T))
        order = [X, G, U, HID, O]
        with nc.Block() as block:

            @block.tensor
            def _(pe):
                pe.wait_ge(rounded[X], FT)
                for r, w in enumerate((wg, wu)):
                    for c, (f, lo, hi) in enumerate(chunks):
                        n = r * len(chunks) + c
                        if n >= 4:
                            pe.wait_ge(kept, n - 3)
                        for k in range(FT):
                            last = pe.matmul(ps[n % 4][:, :], w[:, k, f * P:(f + 1) * P], x_fm[:, k, lo:hi],
                                             start=k == 0, stop=k == FT - 1)
                        last.then_inc(made, 1)

            @block.scalar
            def _(act):
                def add_magic(q, f, dst, src):
                    act.activation(dst, src, ACT.Identity, bias=magic_cell[:, 0:1],
                                   scale=inv[:, q:q + 1]).then_inc(added[q], 1)

                def keep(r, f):
                    for c in range(NCH):
                        n = (r * F0T + f) * NCH + c
                        lo = c * BANK
                        act.wait_ge(made, n + 1)
                        act.activation((gate, up)[r][:, f, lo:lo + BANK], ps[n % 4][:, :],
                                       ACT.Copy).then_inc(kept, 1)

                act.wait_ge(cells, 3 * (X + 1))
                for f in range(FT):
                    add_magic(X, f, x_fm[:, f, :], x_fm[:, f, :])
                for f in range(F0T):
                    keep(0, f)
                act.wait_ge(cells, 3 * (G + 1))
                for f in range(F0T):
                    keep(1, f)
                    add_magic(G, f, gate[:, f, :], gate[:, f, :])
                    act.wait_ge(rounded[G], f + 1)
                    if f >= 2:
                        act.wait_ge(hid_done, f - 1)
                    act.activation(sig[f % 2][:, :], gate[:, f, :], ACT.Sigmoid).then_inc(sig_done, 1)
                    act.wait_ge(sig_done, f + 1)
                    act.activation(sig[f % 2][:, :], sig[f % 2][:, :], ACT.Identity,
                                   bias=magic_cell[:, 0:1], scale=65536.0).then_inc(sig_added, 1)
                act.wait_ge(cells, 3 * (U + 1))
                for f in range(F0T):
                    add_magic(U, f, up[:, f, :], up[:, f, :])
                act.wait_ge(cells, 3 * (HID + 1))
                for f in range(F0T):
                    add_magic(HID, f, gate[:, f, :], gate[:, f, :])
                act.wait_ge(cells, 3 * (O + 1))
                for f in range(F0T):
                    add_magic(O, f, gate[:, f, :], gate[:, f, :])

            @block.vector
            def _(dve):
                def see(q, f, src):
                    dve.tensor_reduce(part[:, q, f:f + 1], src, op=ALU.max, axis=AX.XY if q == X else AX.X,
                                      apply_absolute_value=True).then_inc(seen[q], 1)

                def scales(q, n, unit=1.0):
                    dve.wait_ge(seen[q], n)
                    dve.tensor_reduce(amax[:, q:q + 1], part[:, q, 0:n], op=ALU.max, axis=AX.X).then_inc(own, 1)
                    dve.wait_ge(all_max, order.index(q) + 1)
                    dve.tensor_scalar(scale[:, q:q + 1], wide[:, q:q + 1], unit / QA, 1e-12, ALU.mult,
                                      ALU.max).then_inc(cells, 1)
                    dve.wait_ge(cells, 3 * order.index(q) + 1)
                    dve.reciprocal(inv[:, q:q + 1], scale[:, q:q + 1]).then_inc(cells, 1)
                    dve.wait_ge(cells, 3 * order.index(q) + 2)
                    dve.tensor_scalar(inv[:, q:q + 1], inv[:, q:q + 1], unit, None, ALU.mult).then_inc(cells, 1)

                def take_magic(q, f, t):
                    dve.wait_ge(added[q], f + 1)
                    dve.tensor_scalar(t, t, MAGIC, scale[:, q:q + 1], ALU.subtract, ALU.mult).then_inc(rounded[q], 1)

                see(X, 0, x_tok[:, :, :])
                scales(X, 1)
                for f in range(FT):
                    take_magic(X, f, x_fm[:, f, :])
                for f in range(F0T):
                    dve.wait_ge(kept, (f + 1) * NCH)
                    see(G, f, gate[:, f, :])
                scales(G, F0T)
                for f in range(F0T):
                    take_magic(G, f, gate[:, f, :])
                    dve.wait_ge(kept, (F0T + f + 1) * NCH)
                    see(U, f, up[:, f, :])
                    dve.wait_ge(sig_added, f + 1)
                    dve.tensor_scalar(sig[f % 2][:, :], sig[f % 2][:, :], MAGIC, 65535.0, ALU.subtract,
                                      ALU.min).then_inc(sig_int, 1)
                scales(U, F0T)
                for f in range(F0T):
                    take_magic(U, f, up[:, f, :])
                    dve.wait_ge(hid_done, f + 1)
                    see(HID, f, gate[:, f, :])
                scales(HID, F0T, 1.0 / 65536.0)
                for f in range(F0T):
                    take_magic(HID, f, gate[:, f, :])
                for f in range(F0T):
                    dve.wait_ge(o_done, f + 1)
                    see(O, f, gate[:, f, :])
                scales(O, F0T)
                for f in range(F0T):
                    take_magic(O, f, gate[:, f, :])

            @block.gpsimd
            def _(pool):
                def spread(n):
                    q = order[n]
                    pool.wait_ge(own, n + 1)
                    pool.partition_all_reduce(wide[:, q:q + 1], amax[:, q:q + 1], P, RMAX).then_inc(all_max, 1)

                spread(0)
                spread(1)
                for f in range(F0T):
                    pool.wait_ge(sig_int, f + 1)
                    pool.tensor_tensor(gate[:, f, :], gate[:, f, :], sig[f % 2][:, :],
                                       ALU.mult).then_inc(hid_done, 1)
                spread(2)
                spread(3)
                for f in range(F0T):
                    pool.wait_ge(rounded[HID], f + 1)
                    pool.wait_ge(rounded[U], f + 1)
                    pool.tensor_tensor(gate[:, f, :], gate[:, f, :], up[:, f, :], ALU.mult).then_inc(o_done, 1)
                spread(4)



E = 8
HE = 1024
HET = HE // P
CAP = T // E
CAPT = CAP // P


def route(nc, tag, x_fm, wg, before, ones_sq, slot, back, gate_keep):
    with ExitStack() as st:
        m = Mem(nc, st, tag)
        ps, cum, tot = (m.ps(n, [P, BANK])[:, 0:NT * E].rearrange("p (t e) -> p t e", t=NT)
                        for n in ("logits", "cum", "tot"))
        lg = m.sb("lg", [P, NT, E])
        top = m.sb("top", [P, NT])
        ex = m.sb("ex", [P, NT, E])
        cand = m.sb("cand", [P, NT, E])
        iota = m.sb("iota", [P, NT, E])
        token = m.sb("token", [P, NT])
        pick = m.sb("pick", [P, NT])
        hot = m.sb("hot", [P, NT, E])
        hot_bf = m.sb("hot_bf", [P, NT, E], BF16)
        sums = m.sb("sums", [P, NT])
        gate = m.sb("gate", [P, NT])
        run = m.sb("run", [P, NT, E])
        rank = m.sb("rank", [P, NT])
        keep = m.sb("keep", [P, NT])
        row = m.sb("row", [P, NT])
        alt = m.sb("alt", [P, NT])
        made = m.sem("made")
        counted = m.sem("counted")
        expd = m.sem("expd")
        iotas = m.sem("iotas")
        step = m.sem("step")
        HOT = 9
        with nc.Block() as block:

            @block.gpsimd
            def _(pool):
                pool.iota(iota[:, :, :], [[0, NT], [1, E]], base=0, channel_multiplier=0,
                          allow_small_or_imprecise_dtypes=True).then_inc(iotas, 1)
                pool.iota(token[:, :], [[P, NT]], base=T, channel_multiplier=1,
                          allow_small_or_imprecise_dtypes=True).then_inc(iotas, 1)

            @block.tensor
            def _(pe):
                for t in range(NT):
                    for k in range(FT):
                        last = pe.matmul(ps[:, t, :], x_fm[:, k, t * P:(t + 1) * P], wg[:, k, :],
                                         start=k == 0, stop=k == FT - 1)
                last.then_inc(made, 1)
                pe.wait_ge(step, HOT)
                flat = hot_bf[:, :, :].rearrange("p t e -> p (t e)")
                pe.matmul(cum[:, :, :].rearrange("p t e -> p (t e)"), before[:, :], flat, start=True, stop=True)
                pe.matmul(tot[:, :, :].rearrange("p t e -> p (t e)"), ones_sq[:, :], flat, start=True,
                          stop=True).then_inc(counted, 1)

            @block.scalar
            def _(act):
                act.wait_ge(step, 3)
                act.activation(ex[:, :, :], ex[:, :, :], ACT.Exp).then_inc(expd, 1)

            @block.vector
            def _(dve):
                n = [0]

                def then(ins):
                    n[0] += 1
                    ins.then_inc(step, 1)
                    dve.wait_ge(step, n[0])

                def wide(t):
                    return t[:, :].unsqueeze(2).broadcast_to([P, NT, E])

                dve.wait_ge(made, 1)
                dve.wait_ge(iotas, 2)
                then(dve.tensor_copy(lg[:, :, :], ps[:, :, :]))
                then(dve.tensor_reduce(top[:, :], lg[:, :, :], op=ALU.max, axis=AX.X))
                then(dve.tensor_tensor(ex[:, :, :], lg[:, :, :], wide(top), ALU.subtract))
                then(dve.tensor_tensor(hot[:, :, :], lg[:, :, :], wide(top), ALU.is_ge))
                then(dve.tensor_scalar(cand[:, :, :], iota[:, :, :], -1.0, float(E), ALU.mult, ALU.add))
                then(dve.tensor_tensor(hot[:, :, :], hot[:, :, :], cand[:, :, :], ALU.mult))
                then(dve.tensor_reduce(pick[:, :], hot[:, :, :], op=ALU.max, axis=AX.X))
                then(dve.tensor_tensor(hot[:, :, :], cand[:, :, :], wide(pick), ALU.is_equal))
                then(dve.tensor_copy(hot_bf[:, :, :], hot[:, :, :]))
                assert n[0] == HOT
                dve.wait_ge(expd, 1)
                then(dve.tensor_reduce(sums[:, :], ex[:, :, :], op=ALU.add, axis=AX.X))
                then(dve.reciprocal(gate[:, :], sums[:, :]))
                dve.wait_ge(counted, 1)
                then(dve.memset(run[:, 0, :], 0.0))
                for t in range(1, NT):
                    then(dve.tensor_tensor(run[:, t, :], run[:, t - 1, :], tot[:, t - 1, :], ALU.add))
                then(dve.tensor_tensor(run[:, :, :], run[:, :, :], cum[:, :, :], ALU.add))
                then(dve.tensor_tensor(run[:, :, :], run[:, :, :], hot[:, :, :], ALU.mult))
                then(dve.tensor_reduce(rank[:, :], run[:, :, :], op=ALU.add, axis=AX.X))
                then(dve.tensor_scalar(keep[:, :], rank[:, :], float(CAP), None, ALU.is_lt))
                then(dve.tensor_scalar(row[:, :], pick[:, :], -float(CAP), float(E * CAP), ALU.mult, ALU.add))
                then(dve.tensor_tensor(row[:, :], row[:, :], rank[:, :], ALU.add))
                then(dve.tensor_tensor(row[:, :], row[:, :], keep[:, :], ALU.mult))
                then(dve.tensor_copy(back[:, :], row[:, :]))
                then(dve.tensor_scalar(alt[:, :], keep[:, :], -1.0, 1.0, ALU.mult, ALU.add))
                then(dve.tensor_tensor(alt[:, :], alt[:, :], token[:, :], ALU.mult))
                then(dve.tensor_tensor(row[:, :], row[:, :], alt[:, :], ALU.add))
                then(dve.tensor_copy(slot[:, :], row[:, :]))
                then(dve.tensor_tensor(gate_keep[:, :], gate[:, :], keep[:, :], ALU.mult))


def experts(nc, tag, x_tok, slot, back, gate_keep, w1, w2, rows_dram, res_dram, zero_done, addend, ident):
    with ExitStack() as st:
        m = Mem(nc, st, tag)
        xin = [m.sb(f"xin{b}", [P, CAPT, D]) for b in range(2)]
        xfm = [m.sb(f"xfm{b}", [P, FT, CAP]) for b in range(2)]
        w1s = [m.sb(f"w1_{b}", [P, FT, HE]) for b in range(2)]
        w2s = [m.sb(f"w2_{b}", [P, HET, D]) for b in range(2)]
        hid = [m.sb(f"hid{b}", [P, HET, CAP]) for b in range(2)]
        res = [m.sb(f"res{b}", [P, CAPT, D]) for b in range(2)]
        pt = m.ps("pt", [P, FT, CAP])
        ph = [m.ps(f"ph{b}", [P, BANK])[:, 0:CAP] for b in range(4)]
        pr = [m.ps(f"pr{b}", [P, BANK])[:, 0:D] for b in range(2)]
        sent = m.sem("sent")
        x_in = [m.sem(f"x_in{b}") for b in range(2)]
        w_in = [m.sem(f"w_in{b}") for b in range(2)]
        turned, copied, made, gelued, outed, kept = (
            m.sem(n) for n in ("turned", "copied", "made", "gelued", "outed", "kept"))
        stored = [m.sem(f"stored{b}") for b in range(2)]
        fetched, weighed = m.sem("fetched"), m.sem("weighed")

        def at_least(eng, sem, value):
            if not (isinstance(value, int) and value <= 0):
                eng.wait_ge(sem, value)

        def loop(body):
            def program(eng):
                for e in (0, 1):
                    body(eng, e, 0, e)
                with eng.Fori(1, E // 2) as pair:
                    for b in range(2):
                        body(eng, 2 * pair + b, pair, b)
            return program

        with nc.Block() as block:

            @block.gpsimd
            def _(pool):
                for t in range(NT):
                    pool.indirect_dma_start(out=rows_dram[:, :], out_offset=bass.IndirectOffsetOnAxis(
                        ap=slot[:, t:t + 1], axis=0), in_=x_tok[:, t, :], in_offset=None).then_inc(sent, 16)
                for b in range(2):
                    pool.wait_ge(stored[b], 16 * E // 2)
                for t in range(NT):
                    pool.indirect_dma_start(out=addend[:, t, :], out_offset=None, in_=res_dram[:, :],
                                            in_offset=bass.IndirectOffsetOnAxis(ap=back[:, t:t + 1], axis=0)
                                            ).then_inc(fetched, 16)
                pool.wait_ge(fetched, 16 * NT)
                for t in range(NT):
                    pool.tensor_scalar(addend[:, t, :], addend[:, t, :], gate_keep[:, t:t + 1], None,
                                       ALU.mult).then_inc(weighed, 1)

            @block.sync
            def _(sp):
                def weights(e, b):
                    at_least(sp, outed, (e - 1) * CAPT)
                    sp.dma_start(w1s[b][:, :, :], w1[bass.ds(e * D, D), :].rearrange("(k p) n -> p k n", p=P)
                                 ).then_inc(w_in[b], 16)
                    sp.dma_start(w2s[b][:, :, :], w2[bass.ds(e * HE, HE), :].rearrange("(k p) n -> p k n", p=P)
                                 ).then_inc(w_in[b], 16)

                weights(0, 0)
                weights(1, 1)
                sp.wait_ge(sent, 16 * NT)

                def body(sp, e, pair, b):
                    if not isinstance(e, int):
                        weights(e, b)
                    at_least(sp, turned, e - 1)
                    sp.dma_start(xin[b][:, :, :], rows_dram[bass.ds(e * CAP, CAP), :].rearrange(
                        "(t p) d -> p t d", p=P)).then_inc(x_in[b], 16)

                loop(body)(sp)

            @block.tensor
            def _(pe):
                def body(pe, e, pair, b):
                    pe.wait_ge(x_in[b], 16 * (pair + 1))
                    at_least(pe, copied, e)
                    for k in range(FT):
                        for t in range(CAPT):
                            last = pe.transpose(pt[:, k, t * P:(t + 1) * P], xin[b][:, t, k * P:(k + 1) * P],
                                                ident[:, :])
                    last.then_inc(turned, 1)
                    pe.wait_ge(w_in[b], 32 * (pair + 1))
                    pe.wait_ge(copied, e + 1)
                    for f in range(HET):
                        at_least(pe, gelued, e * HET + f - 3)
                        for k in range(FT):
                            last = pe.matmul(ph[f % 4][:, :], w1s[b][:, k, f * P:(f + 1) * P], xfm[b][:, k, :],
                                             start=k == 0, stop=k == FT - 1)
                        last.then_inc(made, 1)
                    pe.wait_ge(gelued, (e + 1) * HET)
                    for t in range(CAPT):
                        at_least(pe, kept, e * CAPT + t - 1)
                        for f in range(HET):
                            last = pe.matmul(pr[t][:, :], hid[b][:, f, t * P:(t + 1) * P], w2s[b][:, f, :],
                                             start=f == 0, stop=f == HET - 1)
                        last.then_inc(outed, 1)

                loop(body)(pe)

            @block.vector
            def _(dve):
                def body(dve, e, pair, b):
                    dve.wait_ge(turned, e + 1)
                    at_least(dve, made, (e - 1) * HET)
                    dve.tensor_copy(xfm[b][:, :, :], pt[:, :, :]).then_inc(copied, 1)
                    if not isinstance(e, int):
                        dve.wait_ge(stored[b], 16 * pair)
                    for t in range(CAPT):
                        dve.wait_ge(outed, e * CAPT + t + 1)
                        dve.tensor_copy(res[b][:, t, :], pr[t][:, :]).then_inc(kept, 1)

                loop(body)(dve)

            @block.scalar
            def _(act):
                def body(act, e, pair, b):
                    at_least(act, outed, (e - 1) * CAPT)
                    for f in range(HET):
                        act.wait_ge(made, e * HET + f + 1)
                        act.activation(hid[b][:, f, :], ph[f % 4][:, :], ACT.Gelu_apprx_tanh).then_inc(gelued, 1)
                    act.wait_ge(kept, (e + 1) * CAPT)
                    act.dma_start(res_dram[bass.ds(e * CAP, CAP), :].rearrange("(t p) d -> p t d", p=P),
                                  res[b][:, :, :]).then_inc(stored[b], 16)

                loop(body)(act)



CONST32 = ("eye", "neg_eye", "group_mean")
CONST16 = ("eye", "flip", "band_keys", "band_queries", "before", "ones")


def load(nc, tag, pairs):
    with ExitStack() as st:
        done = Mem(nc, st, tag).sem("done")
        with nc.Block() as block:

            @block.sync
            def _(sp):
                for dst, src in pairs:
                    sp.dma_start(dst, src, allow_slow_non_contiguous=True).then_inc(done, 16)
                sp.wait_ge(done, 16 * len(pairs))


def begin_load(nc, triples):
    with nc.Block() as block:

        @block.sync
        def _(sp):
            for dst, src, sem in triples:
                sp.dma_start(dst, src).then_inc(sem, 16)


def in_major(w):
    return w.rearrange("(k p) n -> p k n", p=P)


def column(v):
    return v.rearrange("(f p) -> p f", p=P)


def row_everywhere(v):
    return v.unsqueeze(0).broadcast_to([P, v.shape[0]])


def by_head(v):
    return bass.AP(v.tensor, 0, [[0, P // DH], [1, DH], [1, 1]])


def build_bands(nc, tag, rel, rel_back, band_dram):
    W = 3 * P
    with ExitStack() as st:
        m = Mem(nc, st, tag)
        r = m.sb("r", [H, 2, MAXREL + 1])
        lin = m.sb("lin", [H, 2, W])
        rest = m.sb("rest", [H, 2, W])
        parts = m.sb("parts", [H, 2, PARTS, W], BF16)
        got, step, out = m.sem("got"), m.sem("step"), m.sem("out")
        with nc.Block() as block:

            @block.sync
            def _(sp):
                sp.dma_start(r[:, 0, :], rel).then_inc(got, 16)
                sp.dma_start(r[:, 1, :], rel_back).then_inc(got, 16)
                sp.wait_ge(step, 12)
                sp.dma_start(band_dram, parts[:, :, :, :]).then_inc(out, 16)
                sp.wait_ge(out, 16)

            @block.vector
            def _(dve):
                n = [0]

                def then(ins):
                    n[0] += 1
                    ins.then_inc(step, 1)
                    dve.wait_ge(step, n[0])

                dve.wait_ge(got, 32)
                then(dve.memset(lin[:, 0, 0:P - 1], NEG))
                then(dve.tensor_scalar(lin[:, 0, P - 1:2 * P - 1], r[:, 0, 0:MAXREL], r[:, 0, MAXREL:MAXREL + 1],
                                       None, ALU.subtract))
                then(dve.memset(lin[:, 0, 2 * P - 1:W], 0.0))
                then(dve.memset(lin[:, 1, 0:P], 0.0))
                then(dve.tensor_scalar(lin[:, 1, P:2 * P], r[:, 1, 1:MAXREL + 1], r[:, 1, 0:1], None,
                                       ALU.subtract))
                then(dve.memset(lin[:, 1, 2 * P:W], NEG))
                then(dve.tensor_copy(parts[:, :, 0, :], lin[:, :, :]))
                then(dve.tensor_tensor(rest[:, :, :], lin[:, :, :], parts[:, :, 0, :], ALU.subtract))
                then(dve.tensor_copy(parts[:, :, 1, :], rest[:, :, :]))
                then(dve.tensor_tensor(lin[:, :, :], rest[:, :, :], parts[:, :, 1, :], ALU.subtract))
                then(dve.tensor_copy(parts[:, :, 2, :], lin[:, :, :]))
                then(dve.memset(rest[:, 0, 0:1], 0.0))


def mask_state(nc, tag, largest, flag):
    RMAX = bass.bass_isa.ReduceOp.max
    with ExitStack() as st:
        m = Mem(nc, st, tag)
        own, every = m.sb("own", [P, 1]), m.sb("every", [P, 1])
        reduced, spread, set_ = m.sem("reduced"), m.sem("spread"), m.sem("set")
        with nc.Block() as block:

            @block.vector
            def _(dve):
                dve.tensor_reduce(own[:, :], largest[:, :], op=ALU.max, axis=AX.X).then_inc(reduced, 1)
                dve.wait_ge(spread, 1)
                dve.tensor_scalar(flag[:, :], every[0:1, :], 0.0, None, ALU.is_gt).then_inc(set_, 1)

            @block.gpsimd
            def _(pool):
                pool.wait_ge(reduced, 1)
                pool.partition_all_reduce(every[:, :], own[:, :], P, RMAX).then_inc(spread, 1)


def prepare(nc, tag, steps):
    with ExitStack() as st:
        step = Mem(nc, st, tag).sem("step")
        with nc.Block() as block:

            @block.vector
            def _(dve):
                for n, f in enumerate(steps):
                    f(dve).then_inc(step, 1)
                    dve.wait_ge(step, n + 1)


def decoder(nc, a, out, stop=99, dump=None):
    Mem.retired.clear()
    with ExitStack() as top:
        g = Mem(nc, top, "g")
        x_tok = g.sb("x_tok", [P, NT, D])
        o_tok = g.sb("o_tok", [P, NT, D])
        c32 = g.sb("c32", [P, len(CONST32), P])
        c16 = g.sb("c16", [P, len(CONST16), P], BF16)
        ones = g.sb("ones", [1, P])
        cells = g.sb("cells", [P, 4])
        zero_col, magic_cell, eps_cell = cells[:, 0:2], cells[:, 2:3], cells[:, 3:4]
        eye, neg_eye, group_mean = (c32[:, n, :] for n in range(3))
        eye_bf, flip = c16[:, 0, :], c16[:, 1, :]
        bands = c16[:, 2:4, :]
        before, ones_sq = c16[:, 4, :], c16[:, 5, :]

        q_dram = nc.dram_tensor("q_parts", [D, PARTS, T], BF16).ap()
        k_dram = nc.dram_tensor("k_parts", [D, PARTS, T], BF16).ap()
        kx_dram = nc.dram_tensor("kx_parts", [D, PARTS, TC], BF16).ap()
        band_dram = nc.dram_tensor("bands", [H, 2, PARTS, 3 * P], BF16).ap()
        rows_dram = nc.dram_tensor("expert_rows", [2 * T, D], FP32).ap()
        res_dram = nc.dram_tensor("expert_results", [T, D], FP32).ap()

        def band_of(h, which):
            line = band_dram[bass.ds(h, 1), which, :, 0:2 * P]
            return bass.AP(band_dram.tensor, line.offset, [[1, P], [3 * P, PARTS], [1, 2 * P]])

        x_rows = a["x"][0].rearrange("(t p) d -> p t d", p=P)
        with ExitStack() as st:
            wide16 = Mem(nc, st, "l0w").sb("wide16", [P, len(CONST16), P])
            load(nc, "l0", [(x_tok[:, :, :], x_rows),
                            (c32[:, :, :], a["const32"].rearrange("c p n -> p c n")),
                            (wide16[:, :, :], a["const16"].rearrange("c p n -> p c n"))])
            prepare(nc, "p1", [lambda d: d.tensor_copy(c16[:, :, :], wide16[:, :, :])])
        prepare(nc, "p0", [lambda d: d.memset(ones[:, :], 1.0),
                           lambda d: d.memset(cells[:, 0:2], 0.0),
                           lambda d: d.memset(cells[:, 2:3], MAGIC),
                           lambda d: d.memset(cells[:, 3:4], QN_EPS)])
        build_bands(nc, "bands", a["L0_attn_rel"], a["rel_back"], band_dram)

        fm_spare = o_tok[:, :, :].rearrange("p t d -> p (t d)").rearrange("p (f n) -> p f n", f=FT)

        def close(tag, w_dram, b_dram, resid):
            with ExitStack() as st:
                m = Mem(nc, st, tag)
                fm = m.sb("fm", [P, FT, T])
                w = m.sb("w", [P, FT, D])
                b = m.sb("b", [1, D]) if b_dram is not None else None
                load(nc, tag + "l", [(w[:, :, :], in_major(w_dram))]
                     + ([(b[:, :], b_dram.unsqueeze(0))] if b is not None else []))
                to_feature_major(nc, tag + "t", o_tok, fm, eye)
                project_norm(nc, tag + "n", x_tok, fm, w, b, ones, resid)

        def done(n):
            Mem.reclaim(nc)
            if stop == n:
                load_out(nc, "dump", out, x_tok)
                return True
            return False

        def context(m):
            fm = m.sb("ctx", [P, FT, TC])
            return fm, (fm[:, :, :], in_major(a["ctx_t"]))

        with ExitStack() as st:
            m = Mem(nc, st, "a0")
            v_sb = m.sb("v_sb", [P, NT, D])
            with ExitStack() as inner:
                p = Mem(nc, inner, "a0p")
                fm = p.sb("fm", [P, FT, T])
                w = [p.sb(f"w{n}", [P, FT, D]) for n in range(3)]
                vb = p.sb("vb", [P, D])
                gamma, beta = p.sb("gamma", [P, FT]), p.sb("beta", [P, FT])
                load(nc, "a0l", [(w[n][:, :, :], in_major(a[name])) for n, name in
                                 enumerate(("L0_attn_WqT", "L0_attn_WkT", "L0_attn_WvT"))]
                     + [(gamma[:, :], column(a["L0_attn_ln_gamma"])), (beta[:, :], column(a["L0_attn_ln_beta"]))])
                prepare(nc, "a0m", [lambda d: d.memset(vb[:, :], 0.0)])
                project_norm(nc, "a0n", x_tok, out=o_tok)
                to_feature_major(nc, "a0t", o_tok, fm, eye, gamma, beta)
                project_split(nc, "a0s", [(w[0], fm, T, 0.25, zero_col, q_dram, False),
                                          (w[1], fm, T, 1.0, zero_col, k_dram, True)], (w[2], fm, T, vb, v_sb))
            attention(nc, "a0a", T, "rel", q_dram, k_dram, v_sb, o_tok, eye, flip=flip, band_dram=band_of,
                      ident_bf=eye_bf)
        close("a0c", a["L0_attn_WoT"], None, 2.0)
        if done(0):
            return

        with ExitStack() as st:
            m = Mem(nc, st, "x0")
            v_sb = m.sb("v_sb", [P, CT, D])
            mask_sb = m.sb("mask", [P, NT, TC])
            flag = m.sb("flag", [1, 1], INT32)
            largest = m.sb("largest", [P, NT])
            mask_rows = a["mask_1x1xSxS2_ff0"][0, 0].rearrange("(t p) n -> p t n", p=P)
            with ExitStack() as inner:
                p = Mem(nc, inner, "x0p")
                fm = fm_spare
                ctx, ctx_load = context(p)
                w = [p.sb(f"w{n}", [P, FT, D]) for n in range(3)]
                cols = [p.sb(f"b{n}", [P, FT]) for n in range(2)]
                vb = p.sb("vb", [P, D])
                load(nc, "x0l", [(w[n][:, :, :], in_major(a["L0_xattn_" + k])) for n, k in enumerate(("wq", "wk", "wv"))]
                     + [(cols[n][:, :], column(a["L0_xattn_" + k])) for n, k in enumerate(("bq", "bk"))]
                     + [(vb[:, :], row_everywhere(a["L0_xattn_bv"])), ctx_load])
                mask_in = [p.sem(f"mask_in{n}") for n in range(4)]
                begin_load(nc, [(mask_sb[:, 4 * n:4 * n + 4, :], mask_rows[:, 4 * n:4 * n + 4, :], mask_in[n])
                                for n in range(4)])
                prepare(nc, "x0m", [lambda d: d.tensor_scalar(cols[0][:, :], cols[0][:, :], 0.25, None, ALU.mult)])
                to_feature_major(nc, "x0t", x_tok, fm, eye)
                project_split(nc, "x0s", [(w[0], fm, T, 0.25, cols[0], q_dram, False),
                                          (w[1], ctx, TC, 1.0, cols[1], kx_dram, True)], (w[2], ctx, TC, vb, v_sb),
                              scan=(mask_sb, mask_in, largest))
                mask_state(nc, "x0f", largest, flag)
            attention(nc, "x0a", TC, "mask", q_dram, kx_dram, v_sb, o_tok, eye, mask_sb=mask_sb,
                      mask_flag=flag[0:1, 0:1], neg_eye=neg_eye, ident_bf=eye_bf)
        close("x0c", a["L0_xattn_wo"], a["L0_xattn_bo"], 1.0)
        if done(1):
            return

        with ExitStack() as st:
            m = Mem(nc, st, "f0")
            wd = m.sb("wd", [P, F0T, D])
            gate = m.sb("gate", [P, F0T, T])
            with ExitStack() as inner:
                p = Mem(nc, inner, "f0p")
                fm = fm_spare
                wg, wu = p.sb("wg", [P, FT, F0]), p.sb("wu", [P, FT, F0])
                with ExitStack() as raws:
                    r = Mem(nc, raws, "f0r")
                    raw = [r.sb(f"raw{n}", [P, F0T, D]) for n in range(2)] + [r.sb("raw2", [P, FT, F0])]
                    load(nc, "f0l", [(raw[n][:, :, :], a["L0_ffn_" + k].rearrange("(o p) i -> p o i", p=P))
                                     for n, k in enumerate(("w_gate", "w_up", "w_down"))])
                    for n, (fmw, o, i) in enumerate(((wg, F0, D), (wu, F0, D), (wd, D, F0))):
                        dequantise(nc, f"f0d{n}", raw[n], fmw, eye, o, i)
                to_feature_major(nc, "f0t", x_tok, fm, eye)
                quantised_ffn(nc, "f0q", x_tok, fm, wg, wu, gate, magic_cell)
            project_norm(nc, "f0n", x_tok, gate, wd)
        if done(2):
            return

        with ExitStack() as st:
            m = Mem(nc, st, "a1")
            v_sb = m.sb("v_sb", [P, NT, D])
            with ExitStack() as inner:
                p = Mem(nc, inner, "a1p")
                fm = fm_spare
                w = [p.sb(f"w{n}", [P, FT, D]) for n in range(3)]
                cols = [p.sb(f"b{n}", [P, FT]) for n in range(2)]
                vb = p.sb("vb", [P, D])
                bq = a["L1_attn_b_qkv"]
                load(nc, "a1l", [(w[n][:, :, :], in_major(a["L1_attn_w_qkv"])[:, :, n * D:(n + 1) * D]) for n in range(3)]
                     + [(cols[n][:, :], column(bq[n * D:(n + 1) * D])) for n in range(2)]
                     + [(vb[:, :], row_everywhere(bq[2 * D:3 * D]))])
                prepare(nc, "a1m", [lambda d: d.tensor_scalar(cols[0][:, :], cols[0][:, :], 0.25, None, ALU.mult)])
                to_feature_major(nc, "a1t", x_tok, fm, eye)
                project_split(nc, "a1s", [(w[0], fm, T, 0.25, cols[0], q_dram, False),
                                          (w[1], fm, T, 1.0, cols[1], k_dram, True)], (w[2], fm, T, vb, v_sb))
            attention(nc, "a1a", T, "tri", q_dram, k_dram, v_sb, o_tok, eye, flip=flip, bands=bands,
                      ident_bf=eye_bf)
        close("a1c", a["L1_attn_w_out"], a["L1_attn_b_out"], 1.0)
        if done(3):
            return

        with ExitStack() as st:
            m = Mem(nc, st, "x1")
            v_sb = m.sb("v_sb", [P, CT, D])
            key_row = m.sb("key_row", [1, TC], BF16)
            with ExitStack() as inner:
                p = Mem(nc, inner, "x1p")
                fm = fm_spare
                ctx, ctx_load = context(p)
                qn, kn = p.sb("qn", [P, FT, T]), p.sb("kn", [P, FT, TC])
                w = [p.sb(f"w{n}", [P, FT, D]) for n in range(3)]
                cols = [p.sb(f"b{n}", [P, FT]) for n in range(2)]
                norm = [p.sb(f"n{n}", [P, 1]) for n in range(4)]
                vb = p.sb("vb", [P, D])
                named = p.sb("named", [1, TC], UINT8)
                bkv = a["L1_xattn_bkv"]
                load(nc, "x1l", [(w[0][:, :, :], in_major(a["L1_xattn_WqT"]))]
                     + [(w[n + 1][:, :, :], in_major(a["L1_xattn_WkvT"])[:, :, n * D:(n + 1) * D]) for n in range(2)]
                     + [(cols[0][:, :], column(a["L1_xattn_bq"])), (cols[1][:, :], column(bkv[0:D])),
                        (vb[:, :], row_everywhere(bkv[D:2 * D])), (named[:, :], a["mask_BxS2_bk0"]), ctx_load]
                     + [(norm[n][:, :], by_head(a["L1_xattn_" + k])) for n, k in
                        enumerate(("qn_w", "qn_b", "kn_w", "kn_b"))])
                prepare(nc, "x1m", [lambda d: d.tensor_scalar(key_row[:, :], named[:, :], 1.0, -NEG, ALU.subtract, ALU.mult)])
                to_feature_major(nc, "x1t", x_tok, fm, eye)
                head_norm(nc, "x1h", [(w[0], fm, T, cols[0], norm[0], norm[1], qn),
                                      (w[1], ctx, TC, cols[1], norm[2], norm[3], kn)], group_mean, eps_cell)
                project_split(nc, "x1s", [(None, qn, T, 0.25, zero_col, q_dram, False),
                                          (None, kn, TC, 1.0, zero_col, kx_dram, True)], (w[2], ctx, TC, vb, v_sb))
            attention(nc, "x1a", TC, "row", q_dram, kx_dram, v_sb, o_tok, eye, key_row=key_row[:, :],
                      ident_bf=eye_bf)
        close("x1c", a["L1_xattn_WoT"], a["L1_xattn_bo"], 1.0)
        if done(4):
            return

        with ExitStack() as st:
            m = Mem(nc, st, "e1")
            slot, back = m.sb("slot", [P, NT], mybir.dt.uint32), m.sb("back", [P, NT], mybir.dt.uint32)
            gate_keep = m.sb("gate_keep", [P, NT])
            with ExitStack() as inner:
                p = Mem(nc, inner, "e1p")
                fm = fm_spare
                wg = p.sb("wg", [P, FT, E])
                blank = p.sb("blank", [P, NT, D])
                prepare(nc, "e1z", [lambda d: d.memset(blank[:, :, :], 0.0)])
                load(nc, "e1l", [(wg[:, :, :], in_major(a["L1_ffn_Wg"])),
                                 (rows_dram[0:T, :].rearrange("(t p) d -> p t d", p=P), blank[:, :, :])])
                to_feature_major(nc, "e1t", x_tok, fm, eye)
                route(nc, "e1r", fm, wg, before, ones_sq, slot, back, gate_keep)
            experts(nc, "e1x", x_tok, slot, back, gate_keep, a["L1_ffn_W1"].rearrange("e d n -> (e d) n"),
                    a["L1_ffn_W2"].rearrange("e n d -> (e n) d"), rows_dram, res_dram, None, o_tok, eye)
            project_norm(nc, "e1n", x_tok, addend=o_tok)
        load_out(nc, "out", out, x_tok)


def load_out(nc, tag, out, x_tok):
    with ExitStack() as st:
        done = Mem(nc, st, tag).sem("done")
        with nc.Block() as block:

            @block.sync
            def _(sp):
                sp.dma_start(out[0].rearrange("(t p) d -> p t d", p=P), x_tok[:, :, :]).then_inc(done, 16)
                sp.wait_ge(done, 16)


def host_arrays(inputs):
    import numpy as np

    arrays = {}
    for name, a in inputs.items():
        a = np.asarray(a)
        if name in ("L0_attn_Wq", "L0_attn_Wk", "L0_attn_Wv", "L0_attn_Wo", "L1_xattn_Wq", "L1_xattn_Wkv",
                    "L1_xattn_Wo"):
            name, a = name + "T", a.T
        elif name == "ctx_1024":
            name, a = "ctx_t", a[0].T
        if name == "L0_attn_rel":
            arrays["rel_back"] = np.ascontiguousarray(a[:, ::-1])
        arrays[name] = np.ascontiguousarray(a)
    p, c = np.meshgrid(np.arange(P), np.arange(P), indexing="ij")
    arrays["const32"] = np.stack([np.eye(P), -1e9 * np.eye(P), (p // DH == c // DH) / DH]).astype(np.float32)
    arrays["const16"] = np.stack([np.eye(P), np.eye(P)[::-1], NEG * (p + c < P - 1), NEG * (p + c > P - 1),
                                  p < c, np.ones((P, P))]).astype(np.float32)
    return arrays


def kernel(**inputs):
    import numpy as np
    import concourse.bacc as bacc
    from concourse.bass_utils import run_bass_kernel_spmd

    arrays = host_arrays(inputs)
    nc = bacc.Bacc("TRN2", target_bir_lowering=False, num_devices=1)
    aps, feed = {}, {}
    for name, a in arrays.items():
        feed[f"in_{name}_dram"] = a
        aps[name] = nc.dram_tensor(f"in_{name}_dram", a.shape, mybir.dt.from_np(a.dtype), kind="ExternalInput").ap()
    out = nc.dram_tensor("out_0_dram", (1, T, D), FP32, kind="ExternalOutput").ap()
    decoder(nc, aps, out)
    r = run_bass_kernel_spmd(nc, [feed], core_ids=[0])
    return r.results[0]["out_0_dram"]
```
